# Optimizing a Trainium2 kernel written in Bass

```python
import numpy as np
import jax
import jax.numpy as jnp

def _softmax(x, axis=-1):
    return jax.nn.softmax(x, axis=axis)

def _gelu(x):
    return jax.nn.gelu(x, approximate=True)

def _silu(x):
    return jax.nn.silu(x)

def _sigmoid(x):
    return jax.nn.sigmoid(x)

def _layernorm(x, axis=-1, eps=1e-05):
    m = jnp.mean(x, axis=axis, keepdims=True)
    v = jnp.var(x, axis=axis, keepdims=True)
    return (x - m) / jnp.sqrt(v + eps)

def _scatter_add(tgt, idx, src, axis=0):
    return tgt.at[idx].add(src)

def _segment_sum(src, seg, n):
    return jax.ops.segment_sum(src, seg, n)
kernel_name = 'mk_seq_preln_d1_jaxref_r8_dd4255'

def setup_inputs(seed: int=0):
    np.random.seed(seed)
    _w = jnp.asarray

    def _L0_attn_setup():
        import jax, jax.numpy as jnp
        import numpy as np
        import math
        B_SZ, T, D_IN, D_OUT, N = (8, 512, 128, 128, 64)
        RMIN, RMAX, MAX_PHASE = (0.9, 1.0, 6.283)
        key = jax.random.key(seed)
        ks = jax.random.split(key, 9)
        x = jax.random.normal(ks[0], (B_SZ, T, D_IN), dtype=jnp.float32)
        u1 = jax.random.uniform(ks[1], (N,), dtype=jnp.float32)
        u2 = jax.random.uniform(ks[2], (N,), dtype=jnp.float32)
        nu_log = jnp.log(-0.5 * jnp.log(u1 * (RMAX + RMIN) * (RMAX - RMIN) + RMIN ** 2))
        theta_log = jnp.log(MAX_PHASE * u2)
        lam_mod = jnp.exp(-jnp.exp(nu_log))
        gamma_log = jnp.log(jnp.sqrt(1.0 - jnp.square(lam_mod)))
        B_re = jax.random.normal(ks[3], (N, D_IN), dtype=jnp.float32) / math.sqrt(2 * D_IN)
        B_im = jax.random.normal(ks[4], (N, D_IN), dtype=jnp.float32) / math.sqrt(2 * D_IN)
        C_re = jax.random.normal(ks[5], (D_OUT, N), dtype=jnp.float32) / math.sqrt(N)
        C_im = jax.random.normal(ks[6], (D_OUT, N), dtype=jnp.float32) / math.sqrt(N)
        D = jax.random.normal(ks[7], (D_OUT, D_IN), dtype=jnp.float32) / math.sqrt(D_IN)
        return {'x': x, 'nu_log': nu_log, 'theta_log': theta_log, 'gamma_log': gamma_log, 'B_re': B_re, 'B_im': B_im, 'C_re': C_re, 'C_im': C_im, 'D': D}
    _L0_attn_in = _L0_attn_setup()

    def _L0_ffn_setup():
        import jax, jax.numpy as jnp
        import numpy as np
        B, T, C = (2, 64, 128)
        I = 512
        E = 8
        K = 2
        key = jax.random.key(seed)
        ks = jax.random.split(key, 8)
        s = 0.02
        return {'x': jax.random.normal(ks[0], (B, T, C), jnp.float32), 'Wr1': jax.random.normal(ks[1], (C, C // 4), jnp.float32) * s, 'br1': jnp.zeros((C // 4,), jnp.float32), 'Wr2': jax.random.normal(ks[2], (C // 4, E), jnp.float32) * s, 'br2': jnp.zeros((E,), jnp.float32), 'Ws1': jax.random.normal(ks[3], (C, I), jnp.float32) * s, 'bs1': jnp.zeros((I,), jnp.float32), 'Ws2': jax.random.normal(ks[4], (I, C), jnp.float32) * s, 'bs2': jnp.zeros((C,), jnp.float32), 'We1': jax.random.normal(ks[5], (E, C, I), jnp.float32) * s, 'be1': jnp.zeros((E, I), jnp.float32), 'We2': jax.random.normal(ks[6], (E, I, C), jnp.float32) * s, 'be2': jnp.zeros((E, C), jnp.float32)}
    _L0_ffn_in = _L0_ffn_setup()
    _d = {'L0_attn_x': _L0_attn_in['x'], 'L0_attn_nu_log': _L0_attn_in['nu_log'], 'L0_attn_theta_log': _L0_attn_in['theta_log'], 'L0_attn_gamma_log': _L0_attn_in['gamma_log'], 'L0_attn_B_re': _L0_attn_in['B_re'], 'L0_attn_B_im': _L0_attn_in['B_im'], 'L0_attn_C_re': _L0_attn_in['C_re'], 'L0_attn_C_im': _L0_attn_in['C_im'], 'L0_attn_D': _L0_attn_in['D'], 'L0_ffn_Wr1': _L0_ffn_in['Wr1'], 'L0_ffn_br1': _L0_ffn_in['br1'], 'L0_ffn_Wr2': _L0_ffn_in['Wr2'], 'L0_ffn_br2': _L0_ffn_in['br2'], 'L0_ffn_Ws1': _L0_ffn_in['Ws1'], 'L0_ffn_bs1': _L0_ffn_in['bs1'], 'L0_ffn_Ws2': _L0_ffn_in['Ws2'], 'L0_ffn_bs2': _L0_ffn_in['bs2'], 'L0_ffn_We1': _L0_ffn_in['We1'], 'L0_ffn_be1': _L0_ffn_in['be1'], 'L0_ffn_We2': _L0_ffn_in['We2'], 'L0_ffn_be2': _L0_ffn_in['be2']}
    _x0 = _d['L0_attn_x']
    _d['L0_attn_x'] = jax.random.normal(jax.random.fold_in(jax.random.key(seed), 1), (2, 1024, 128), dtype=_x0.dtype)
    del _x0
    return _d

def reference(L0_attn_x, L0_attn_nu_log, L0_attn_theta_log, L0_attn_gamma_log, L0_attn_B_re, L0_attn_B_im, L0_attn_C_re, L0_attn_C_im, L0_attn_D, L0_ffn_Wr1, L0_ffn_br1, L0_ffn_Wr2, L0_ffn_br2, L0_ffn_Ws1, L0_ffn_bs1, L0_ffn_Ws2, L0_ffn_bs2, L0_ffn_We1, L0_ffn_be1, L0_ffn_We2, L0_ffn_be2):

    def _L0_attn_ref(x, nu_log, theta_log, gamma_log, B_re, B_im, C_re, C_im, D):
        import jax, jax.numpy as jnp
        import numpy as np
        import math
        B_SZ, T, D_IN, D_OUT, N = (8, 512, 128, 128, 64)
        RMIN, RMAX, MAX_PHASE = (0.9, 1.0, 6.283)
        lam = jnp.exp(-jnp.exp(nu_log) + 1j * jnp.exp(theta_log))
        gamma = jnp.exp(gamma_log)
        Bmat = B_re + 1j * B_im
        Bu = jnp.einsum('bti,ni->btn', x.astype(Bmat.dtype), Bmat) * gamma
        A = jnp.broadcast_to(lam, Bu.shape)

        def combine(e1, e2):
            a1, b1 = e1
            a2, b2 = e2
            return (a1 * a2, a2 * b1 + b2)
        _, states = jax.lax.associative_scan(combine, (A, Bu), axis=1)
        Cmat = C_re + 1j * C_im
        y = jnp.einsum('btn,on->bto', states, Cmat).real + jnp.einsum('bti,oi->bto', x, D)
        return y

    def _L0_ffn_ref(x, Wr1, br1, Wr2, br2, Ws1, bs1, Ws2, bs2, We1, be1, We2, be2):
        import jax, jax.numpy as jnp
        import numpy as np
        B, T, C = (2, 64, 128)
        I = 512
        E = 8
        K = 2
        Bb, Tt, Cc = x.shape
        xf = x.reshape(-1, Cc)
        logits = jax.nn.relu(xf @ Wr1 + br1) @ Wr2 + br2
        gates = jax.nn.softmax(logits, axis=-1)
        tg, ti = jax.lax.top_k(gates, K)
        tg = jax.nn.softmax(tg / K, axis=-1)
        out = jax.nn.silu(xf @ Ws1 + bs1) @ Ws2 + bs2
        for e in range(E):
            h = jax.nn.silu(xf @ We1[e] + be1[e]) @ We2[e] + be2[e]
            w = jnp.sum(tg * (ti == e), axis=-1)
            out = out + w[:, None] * h
        return out.reshape(Bb, Tt, Cc)
    x = L0_attn_x
    x = x + _L0_attn_ref(_layernorm(x, axis=-1), L0_attn_nu_log, L0_attn_theta_log, L0_attn_gamma_log, L0_attn_B_re, L0_attn_B_im, L0_attn_C_re, L0_attn_C_im, L0_attn_D)
    x = x + _L0_ffn_ref(_layernorm(x, axis=-1), L0_ffn_Wr1, L0_ffn_br1, L0_ffn_Wr2, L0_ffn_br2, L0_ffn_Ws1, L0_ffn_bs1, L0_ffn_Ws2, L0_ffn_bs2, L0_ffn_We1, L0_ffn_be1, L0_ffn_We2, L0_ffn_be2)
    return x

_drawn_inputs = setup_inputs


def setup_inputs(seed=0):
    import zlib

    import numpy as np

    out = dict(_drawn_inputs(seed))
    spreads = {'L0_ffn_br1': (0.0, 0.666),
     'L0_ffn_br2': (0.0, 0.1),
     'L0_ffn_bs1': (0.0, 0.566),
     'L0_ffn_bs2': (0.0, 0.1),
     'L0_ffn_be1': (0.0, 0.8),
     'L0_ffn_be2': (0.0, 0.1)}
    factors = {'L0_ffn_Wr1': 3.188}
    for name, (base, spread) in spreads.items():
        noise = np.random.default_rng([zlib.crc32(name.encode()), seed]).standard_normal(out[name].shape)
        drawn = base * np.exp(spread * noise) if base else spread * noise
        out[name] = jnp.asarray(drawn.astype(out[name].dtype))
    for name, factor in factors.items():
        out[name] = (out[name] * factor).astype(out[name].dtype)
    return out
```

```python
from contextlib import ExitStack

import concourse.bass as bass
from concourse import mybir

F32 = mybir.dt.float32
BF16 = mybir.dt.bfloat16
I32 = mybir.dt.int32
U32 = mybir.dt.uint32
ALU = mybir.AluOpType
ACT = mybir.ActivationFunctionType
AX = mybir.AxisListType

P = 128
TILES = 16
GROUPS = 4
TG = TILES // GROUPS
GT = TG * P
SEQ_GROUPS = 2
NS = 64
C = 128
I = 512
IC = I // P
E = 8
K = 2
R = 32
TOKENS = TILES * P
BLOCKS = K * TILES
UNITS = K * TOKENS // P + E - 1
RING = 3
ROUNDS = UNITS // RING
FINE = 32
COARSE = GT // FINE
OW2, OB1, OB2, WCOLS = I, 2 * I, 2 * I + IC, 2 * I + IC + C
EPS = 1e-5
ROUND = 12582912.0
TWO_PI_HI, TWO_PI_LO = 6.28125, 0.0019353071795864769
PI_DOWN = 3.1415925
assert UNITS % RING == 0


def seq_moe_kernel(nc, x, prm, bt, ct, dt, wr1, br1, wr2, shw, bs2, exw, be2, out):
    xn_dram = nc.dram_tensor("xn_rows", [TOKENS, C], F32, kind="Internal").ap()
    y_dram = nc.dram_tensor("y_rows", [K * TOKENS + UNITS * P, C], F32, kind="Internal").ap()

    with ExitStack() as ctx:
        def sb(name, shape, dtype=F32):
            return ctx.enter_context(nc.sbuf_tensor(name, shape, dtype))

        def sem(name):
            return ctx.enter_context(nc.semaphore(name))

        ident = sb("ident", [P, P])
        before = sb("before", [P, P], BF16)
        ones = sb("ones", [P, P], BF16)
        swap = sb("swap", [P, P])
        row_iota = sb("row_iota", [P, P])
        unit_iota = sb("unit_iota", [P, UNITS + 2])
        block_iota = sb("block_iota", [P, BLOCKS])
        part_iota = sb("part_iota", [P, 1])
        step_iota = sb("step_iota", [P, TOKENS // P])
        spare_iota = sb("spare_iota", [P, UNITS])
        rank_iota = sb("rank_iota", [P, E])
        restart = sb("restart", [P, E, BLOCKS])
        euler = sb("euler", [P, 1])
        inv_euler = sb("inv_euler", [P, 1])
        neg_half = sb("neg_half", [P, TG])
        sign = sb("sign", [P, 1])
        half_pi = sb("half_pi", [P, 1])
        prm_s = sb("prm_s", [P, 3])
        bt_s = sb("bt_s", [P, 2, P])
        ct_s = sb("ct_s", [P, 2, C])
        cw = sb("cw", [P, 2, C])
        dt_s = sb("dt_s", [P, C])
        wr1_s = sb("wr1_s", [P, R])
        br1_s = sb("br1_s", [R, 1])
        wr2_s = sb("wr2_s", [R + 1, E])
        shw_s = sb("shw_s", [P, OB2])
        bs2_s = sb("bs2_s", [P, C])
        exw_s = sb("exw_s", [P, E * WCOLS])
        pw = sb("pw", [P, 5])
        ang = sb("ang", [P, 8])
        fine = sb("fine", [P, 2, FINE])
        coarse = sb("coarse", [P, 2, COARSE + 1])
        coarse_done = sb("coarse_done", [P, 1])
        ftmp = sb("ftmp", [P, 2, FINE])
        cos = sb("cos", [P, GT])
        sin = sb("sin", [P, GT])
        cos_t = sb("cos_t", [P, GT])
        sin_t = sb("sin_t", [P, GT])
        carry = sb("carry", [P, P])
        xs = sb("xs", [P, TILES, C])
        xn = sb("xn", [P, TILES, C])
        xnt = sb("xnt", [P, TOKENS])
        x1 = sb("x1", [P, TILES, C])
        acc = sb("acc", [P, TILES, C])
        xn2t = sb("xn2t", [P, TOKENS])
        bn = sb("bn", [P, 2, TILES, 6])
        mv = sb("mv", [P, 2, TILES, 2])
        veps = sb("veps", [P, 2, TILES])
        rstd = sb("rstd", [P, 2, TILES])
        nmr = sb("nmr", [P, 2, TILES])
        t1 = sb("t1", [P, GROUPS, GT])
        t2 = sb("t2", [P, GROUPS, GT])
        zs = sb("zs", [P, GROUPS, GT])
        h1 = sb("h1", [R + 1, TOKENS])
        lg = sb("lg", [P, TILES, E])
        lmax = sb("lmax", [P, TILES])
        gates = sb("gates", [P, TILES, E])
        rest = sb("rest", [P, TILES, E])
        pick = sb("pick", [P, TILES, E])
        gsum = sb("gsum", [P, TILES])
        ginv = sb("ginv", [P, TILES])
        top = sb("top", [P, K, TILES])
        key = sb("key", [P, TILES])
        wk = sb("wk", [P, K, TILES])
        wtmp = sb("wtmp", [P, 3, TILES])
        chosen = sb("chosen", [P, K, TILES, E], BF16)
        upto = sb("upto", [P, E, BLOCKS])
        posn = sb("posn", [P, E, BLOCKS])
        full = sb("full", [P, E, 16])
        units = sb("units", [P, E])
        units_to = sb("units_to", [P, E])
        first = sb("first", [P, E])
        pos = sb("pos", [P, BLOCKS])
        pos_i = sb("pos_i", [P, BLOCKS], I32)
        pu_i = sb("pu_i", [P, BLOCKS], I32)
        pr_i = sb("pr_i", [P, BLOCKS], I32)
        pu = sb("pu", [P, BLOCKS])
        pr = sb("pr", [P, BLOCKS])
        in_row = sb("in_row", [P, BLOCKS, P], BF16)
        in_unit = sb("in_unit", [P, BLOCKS, UNITS], BF16)
        from_who = sb("from_who", [P, BLOCKS, 2, UNITS], BF16)
        inv = sb("inv", [P, 2, UNITS])
        spare = sb("spare", [P, UNITS])
        dest = sb("dest", [P, UNITS])
        dest_u = sb("dest_u", [P, UNITS], U32)
        tok_u = sb("tok_u", [P, UNITS], U32)
        past = sb("past", [1, UNITS + 2, E])
        who = sb("who", [1, UNITS + 2])
        who_i = sb("who_i", [1, 4 * ROUNDS], I32)
        who0_i = sb("who0_i", [1, 4], I32)
        hs = sb("hs", [P, 2, IC, GT])
        wring = sb("wring", [P, RING, WCOLS])
        xg = sb("xg", [P, RING, C])
        xgt = sb("xgt", [P, RING, P])
        he = sb("he", [P, RING, IC, P])
        ys = sb("ys", [P, RING, C])
        yk = [t[:].rearrange("p g (i c) -> p (g i) c", c=C) for t in (t1, t2)]

        bank = [ctx.enter_context(nc.psum_tensor(f"bank{i}", [P, GT], F32)) for i in range(8)]
        HB = bank[0:3]
        HU = [(bank[0], bank[7]), (bank[1], bank[6]), (bank[2], bank[5])]
        TB, YB = bank[3], bank[4]
        YF = bank[5:7]
        LB = bank[7]

        ld_x = [sem(f"ld_x{g}") for g in range(GROUPS)]
        ld_prm, ld_b, ld_c, ld_r, ld_sh, ld_ex = (sem(n) for n in ("ld_prm", "ld_b", "ld_c", "ld_r", "ld_sh", "ld_ex"))
        cst, powed, sined, angled, tabled, sin_made = (sem(n) for n in ("cst", "powed", "sined", "angled", "tabled", "sin_made"))
        stats1, rstd1, nmr1, xn1_made, t1_done, xnt_made = (sem(n) for n in ("stats1", "rstd1", "nmr1", "xn1_made", "t1_done", "xnt_made"))
        bu_done, turned, v_made, scanned, u1_made, u2_made, carried = (sem(n) for n in ("bu_done", "turned", "v_made", "scanned", "u1_made", "u2_made", "carried"))
        y_done, x1_made, stats2, rstd2, nmr2, xn2_made, t2_done, xn2t_made = (sem(n) for n in ("y_done", "x1_made", "stats2", "rstd2", "nmr2", "xn2_made", "t2_done", "xn2t_made"))
        acc_made, h1_done, h1_made, lg_done, xn_stored = (sem(n) for n in ("acc_made", "h1_done", "h1_made", "lg_done", "xn_stored"))
        dve, lmaxed, exped, wexp, routed, prefixed, posed, who_made, rows_made, inv_done, idx_made = (
            sem(n) for n in ("dve", "lmaxed", "exped", "wexp", "routed", "prefixed", "posed", "who_made", "rows_made", "inv_done", "idx_made"))
        blocks_made = sem("blocks_made")
        sh1, sh_act, sh2, sh_added = (sem(n) for n in ("sh1", "sh_act", "sh2", "sh_added"))
        gathered = [sem(f"gathered{b}") for b in range(RING)]
        scattered = [sem(f"scattered{b}") for b in range(RING)]
        turned_x, xgt_made, s1_done, h_made, s2_done, ys_made, w_set = (
            sem(n) for n in ("turned_x", "xgt_made", "s1_done", "h_made", "s2_done", "ys_made", "w_set"))
        ld_y = [sem(f"ld_y{g}") for g in range(GROUPS)]
        summed, stored = sem("summed"), sem("stored")

        CONSTS = 20
        y_view = y_dram[0:K * TOKENS, :].rearrange("(k i p) c -> p k i c", k=K, p=P)
        x_view = x.rearrange("b (i p) c -> p (b i) c", p=P)
        out_view = out.rearrange("b (i p) c -> p (b i) c", p=P)
        xn_view = xn_dram.rearrange("(i p) c -> p i c", p=P)

        def tiles(g):
            return slice(TG * g, TG * g + TG)

        def toks(g):
            return slice(GT * g, GT * g + GT)

        block = ctx.enter_context(nc.Block())

        @block.sync
        def _(sp):
            sp.dma_start(prm_s[:], prm).then_inc(ld_prm, 16)
            for g in range(GROUPS):
                sp.dma_start(xs[:, tiles(g), :], x_view[:, tiles(g), :]).then_inc(ld_x[g], 16)
                if g == 0:
                    sp.dma_start(bt_s[:], bt).then_inc(ld_b, 16)
            sp.dma_start(ct_s[:], ct).then_inc(ld_c, 16)
            sp.dma_start(dt_s[:], dt).then_inc(ld_c, 16)
            sp.dma_start(wr1_s[:], wr1).then_inc(ld_r, 16)
            sp.dma_start(br1_s[:], br1).then_inc(ld_r, 16)
            sp.dma_start(wr2_s[:], wr2).then_inc(ld_r, 16)
            sp.dma_start(bs2_s[:], bs2.broadcast_to([P, C])).then_inc(ld_sh, 16)
            sp.dma_start(shw_s[:], shw).then_inc(ld_sh, 16)
            ex = exw_s[:].rearrange("p (e w) -> p e w", e=E)
            sp.dma_start(ex[:, :, OB2:], be2.broadcast_to([P, E, C])).then_inc(ld_ex, 16)
            sp.dma_start(ex[:, :, 0:OB2], exw).then_inc(ld_ex, 16)
            for g in range(GROUPS):
                sp.wait_ge(xn2_made, TG * (g + 1))
                sp.dma_start(xn_view[:, tiles(g), :], xn[:, tiles(g), :]).then_inc(xn_stored, 16)
            for b in range(RING):
                sp.wait_ge(scattered[b], 16 * ROUNDS)
            for g in range(GROUPS):
                for k in range(K):
                    sp.dma_start(yk[k][:, tiles(g), :], y_view[:, k, tiles(g), :]).then_inc(ld_y[g], 16)
            for g in range(GROUPS):
                sp.wait_ge(summed, TG * (g + 1))
                sp.dma_start(out_view[:, tiles(g), :], acc[:, tiles(g), :]).then_inc(stored, 16)
            sp.wait_ge(stored, 16 * GROUPS)
            sp.wait_ge(xn_stored, 16 * GROUPS)

        @block.gpsimd
        def _(pool):
            pool.memset(euler[:], 2.718281828459045).then_inc(cst, 1)
            pool.memset(inv_euler[:], 0.36787944117144233).then_inc(cst, 1)
            pool.memset(neg_half[:], -0.5).then_inc(cst, 1)
            pool.memset(half_pi[:], 1.5707963267948966).then_inc(cst, 1)
            pool.wait_ge(ld_prm, 16)
            pool.wait_ge(cst, 4)
            pool.tensor_tensor(pw[:, 0:1], euler[:], prm_s[:, 1:2], ALU.pow).then_inc(powed, 1)
            pool.tensor_tensor(pw[:, 1:2], euler[:], prm_s[:, 0:1], ALU.pow).then_inc(powed, 1)
            pool.tensor_tensor(pw[:, 3:4], euler[:], prm_s[:, 2:3], ALU.pow).then_inc(powed, 1)
            pool.wait_ge(powed, 3)
            pool.tensor_tensor(pw[:, 2:3], inv_euler[:], pw[:, 1:2], ALU.pow).then_inc(powed, 1)
            pool.memset(ident[:], 0.0).then_inc(cst, 1)
            pool.wait_ge(cst, 5)
            pool.affine_select(out=ident[:], in_=ident[:], compare_op=ALU.not_equal, fill=1.0, base=0,
                               pattern=[[-1, P]], channel_multiplier=1).then_inc(cst, 1)

            def rstd_of(n, g, signal, ready):
                pool.wait_ge(ready, g + 1)
                pool.tensor_tensor(rstd[:, n, tiles(g)], veps[:, n, tiles(g)], neg_half[:], ALU.pow).then_inc(signal, 1)

            def add_v(g):
                pool.wait_ge(turned, 2 * (g + 1))
                pool.tensor_tensor(t1[:, g, :], t1[:, g, :], t2[:, g, :], ALU.add).then_inc(v_made, 1)

            def turn_back(g):
                pool.wait_ge(scanned, g + 1)
                pool.tensor_tensor(t2[:, g, :], sin[:], zs[:, g, :], ALU.mult).then_inc(u2_made, 1)

            def start_acc(g):
                if g == 0:
                    pool.wait_ge(ld_sh, 32)
                pool.wait_ge(x1_made, g + 1)
                pool.tensor_tensor(acc[:, tiles(g), :], x1[:, tiles(g), :],
                                   bs2_s[:, None, :].broadcast_to([P, TG, C]), ALU.add).then_inc(acc_made, 1)

            rstd_of(0, 0, rstd1, stats1)
            pool.memset(swap[:], 0.0).then_inc(cst, 1)
            pool.wait_ge(cst, 7)
            pool.affine_select(out=swap[:], in_=swap[:], compare_op=ALU.not_equal, fill=1.0, base=NS,
                               pattern=[[-1, P]], channel_multiplier=1).then_inc(cst, 1)
            pool.wait_ge(cst, 8)
            pool.affine_select(out=swap[:], in_=swap[:], compare_op=ALU.not_equal, fill=-1.0, base=-NS,
                               pattern=[[-1, P]], channel_multiplier=1).then_inc(cst, 1)
            pool.wait_ge(tabled, 1)
            shape = [P, COARSE, FINE]
            cc, cs = (coarse[:, n, 0:COARSE][:, :, None].broadcast_to(shape) for n in (0, 1))
            fc, fs = (fine[:, n, None, :].broadcast_to(shape) for n in (0, 1))
            grid = [t[:].rearrange("p (m j) -> p m j", j=FINE) for t in (sin, sin_t)]
            pool.tensor_tensor(grid[0], cc, fs, ALU.mult).then_inc(sin_made, 1)
            pool.tensor_tensor(grid[1], cs, fc, ALU.mult).then_inc(sin_made, 1)
            pool.wait_ge(sin_made, 2)
            pool.tensor_tensor(sin[:], sin[:], sin_t[:], ALU.add).then_inc(sin_made, 1)
            pool.memset(ones[:], 1.0).then_inc(cst, 1)
            pool.wait_ge(cst, 10)
            pool.affine_select(out=before[:], in_=ones[:], compare_op=ALU.is_gt, fill=0.0, base=0,
                               pattern=[[1, P]], channel_multiplier=-1).then_inc(cst, 1)
            for t, n, step, base, cm in (
                (row_iota, P, 1, 0, 0), (unit_iota, UNITS + 2, 1, 0, 0), (block_iota, BLOCKS, 1, 1, 0),
                (part_iota, 1, 1, 0, 1), (step_iota, TOKENS // P, P, 0, 0),
                (spare_iota, UNITS, P, K * TOKENS + P, 1), (rank_iota, E, -1, E, 0),
            ):
                pool.iota(t[:], [[step, n]], base=base, channel_multiplier=cm,
                          allow_small_or_imprecise_dtypes=True).then_inc(cst, 1)
            pool.memset(restart[:], 1.0).then_inc(cst, 1)
            pool.wait_ge(cst, 19)
            pool.memset(restart[:, :, 0:1], 0.0).then_inc(cst, 1)
            for k in range(1, GROUPS + 2):
                if k < GROUPS:
                    rstd_of(0, k, rstd1, stats1)
                if k - 1 < GROUPS:
                    add_v(k - 1)
                if k >= 2:
                    rstd_of(1, k - 2, rstd2, stats2)
                    start_acc(k - 2)
                if k - 1 < GROUPS:
                    turn_back(k - 1)

            pool.wait_ge(rows_made, 1)
            pool.tensor_tensor(from_who[:, :, 1, :], in_unit[:],
                               block_iota[:, :, None].broadcast_to([P, BLOCKS, UNITS]), ALU.mult).then_inc(blocks_made, 1)

            def gather(u):
                b = u % RING
                if u == 0:
                    pool.wait_ge(idx_made, 2)
                    pool.wait_ge(xn_stored, 16 * GROUPS)
                if u >= RING:
                    pool.wait_ge(turned_x, u - RING + 1)
                pool.indirect_dma_start(xg[:, b, :], None, xn_dram,
                                        bass.IndirectOffsetOnAxis(tok_u[:, u:u + 1], 0)).then_inc(gathered[b], 16)

            def scatter(u):
                b = u % RING
                pool.wait_ge(ys_made, u + 1)
                pool.indirect_dma_start(y_dram, bass.IndirectOffsetOnAxis(dest_u[:, u:u + 1], 0),
                                        ys[:, b, :], None).then_inc(scattered[b], 16)

            for u in range(UNITS + RING):
                if u < UNITS:
                    gather(u)
                if u >= RING:
                    scatter(u - RING)

        @block.scalar
        def _(act):
            act.wait_ge(angled, 1)
            act.wait_ge(cst, 4)
            act.activation(fine[:, 1, 0:1], ang[:, 3:4], ACT.Sin).then_inc(sined, 1)
            act.activation(fine[:, 0, 0:1], ang[:, 4:5], ACT.Sin, bias=half_pi[:], scale=-1.0).then_inc(sined, 1)

            def normalize(n, g, src, ready, signal):
                act.wait_ge(ready, g + 1)
                for i in range(TG * g, TG * g + TG):
                    act.activation(xn[:, i, :], src[:, i, :], ACT.Identity, bias=nmr[:, n, i:i + 1],
                                   scale=rstd[:, n, i:i + 1]).then_inc(signal, 1)

            for k in range(GROUPS + 2):
                if k < GROUPS:
                    normalize(0, k, xs, nmr1, xn1_made)
                    act.wait_ge(t1_done, k + 1)
                    act.copy(xnt[:, toks(k)], TB[:]).then_inc(xnt_made, 1)
                if k >= 2:
                    g = k - 2
                    normalize(1, g, x1, nmr2, xn2_made)
                    act.wait_ge(t2_done, g + 1)
                    act.copy(xn2t[:, toks(g)], YB[:]).then_inc(xn2t_made, 1)
                    act.wait_ge(h1_done, g + 1)
                    if g == 0:
                        act.wait_ge(ld_r, 48)
                    act.activation(h1[0:R, toks(g)], HB[2][0:R, :], ACT.Relu, bias=br1_s[:]).then_inc(h1_made, 1)

            act.wait_ge(lmaxed, 1)
            act.activation(gates[:], lg[:], ACT.Exp).then_inc(exped, 1)
            act.wait_ge(wexp, 1)
            act.activation(wtmp[:, 1, :], wtmp[:, 0, :], ACT.Exp, scale=0.5).then_inc(exped, 1)

            for g in range(GROUPS):
                for c in range(IC):
                    n = g * IC + c
                    act.wait_ge(sh1, n + 1)
                    if g >= 2:
                        act.wait_ge(sh2, g - 1)
                    act.activation(hs[:, g % 2, c, :], HB[n % 3][:], ACT.Silu,
                                   bias=shw_s[:, OB1 + c:OB1 + c + 1]).then_inc(sh_act, 1)

            with act.Fori(0, ROUNDS) as it:
                for b in range(RING):
                    for c in range(IC):
                        if c % 2 == 0:
                            act.wait_ge(s1_done, (it * RING + b) * 2 + c // 2 + 1)
                        act.activation(he[:, b, c, :], HU[b][c // 2][:, c % 2 * P:c % 2 * P + P], ACT.Silu,
                                       bias=wring[:, b, OB1 + c:OB1 + c + 1]).then_inc(h_made, 1)

        @block.vector
        def _(v):
            links = [0]

            def link(ins):
                links[0] += 1
                ins.then_inc(dve, 1)
                v.wait_ge(dve, links[0])

            def stats(n, g, src, signal):
                for i in range(TG * g, TG * g + TG):
                    ins = v.bn_stats(bn[:, n, i, :], src[:, i, :])
                link(ins)
                for i in range(TG * g, TG * g + TG):
                    ins = v.bn_aggr(mv[:, n, i, :], bn[:, n, i, :])
                link(ins)
                v.tensor_scalar(veps[:, n, tiles(g)], mv[:, n, tiles(g), 1], EPS, None, ALU.add).then_inc(signal, 1)

            def offset(n, g, ready, signal):
                v.wait_ge(ready, g + 1)
                v.scalar_tensor_tensor(nmr[:, n, tiles(g)], mv[:, n, tiles(g), 0], -1.0, rstd[:, n, tiles(g)],
                                       ALU.mult, ALU.mult).then_inc(signal, 1)

            v.memset(h1[R:R + 1, :], 1.0)
            v.memset(sign[0:NS, :], 1.0)
            v.memset(sign[NS:P, :], -1.0)
            v.memset(coarse[:, 0, 0:1], 1.0)
            link(v.memset(coarse[:, 1, 0:1], 0.0))
            v.wait_ge(powed, 1)
            link(v.tensor_scalar(ang[:, 0:1], pw[:, 0:1], 0.15915494309189535, ROUND, ALU.mult, ALU.add))
            link(v.tensor_scalar(ang[:, 0:1], ang[:, 0:1], ROUND, None, ALU.subtract))
            link(v.scalar_tensor_tensor(ang[:, 1:2], ang[:, 0:1], -TWO_PI_HI, pw[:, 0:1], ALU.mult, ALU.add))
            link(v.scalar_tensor_tensor(ang[:, 2:3], ang[:, 0:1], -TWO_PI_LO, ang[:, 1:2], ALU.mult, ALU.add))
            link(v.tensor_scalar(ang[:, 3:4], ang[:, 2:3], PI_DOWN, -PI_DOWN, ALU.min, ALU.max))
            v.scalar_tensor_tensor(ang[:, 4:5], ang[:, 3:4], -1.0, ang[:, 3:4], ALU.mult, ALU.max).then_inc(angled, 1)
            v.wait_ge(ld_x[0], 16)
            stats(0, 0, xs, stats1)
            v.wait_ge(sined, 2)

            def double(tab, n, at, c0):
                c, s = tab[:, 0, at:at + 1], tab[:, 1, at:at + 1]
                lo, hi = slice(c0, c0 + n), slice(c0 + n, c0 + 2 * n)
                v.tensor_scalar(ftmp[:, 0, 0:n], tab[:, 1, lo], s, None, ALU.mult)
                link(v.tensor_scalar(ftmp[:, 1, 0:n], tab[:, 0, lo], s, None, ALU.mult))
                v.scalar_tensor_tensor(tab[:, 0, hi], tab[:, 0, lo], c, ftmp[:, 0, 0:n], ALU.mult, ALU.subtract)
                link(v.scalar_tensor_tensor(tab[:, 1, hi], tab[:, 1, lo], c, ftmp[:, 1, 0:n], ALU.mult, ALU.add))

            n = 1
            while n < FINE:
                double(fine, n, n - 1, 0)
                n *= 2
            link(v.tensor_copy(coarse[:, :, 1:2], fine[:, :, FINE - 1:FINE]))
            n = 1
            while n < COARSE:
                double(coarse, n, n, 1)
                n *= 2
            v.tensor_copy(coarse_done[:], coarse[:, 0, 0:1]).then_inc(tabled, 1)
            offset(0, 0, rstd1, nmr1)
            shape = [P, COARSE, FINE]
            cc, cs = (coarse[:, m, 0:COARSE][:, :, None].broadcast_to(shape) for m in (0, 1))
            fc, fs = (fine[:, m, None, :].broadcast_to(shape) for m in (0, 1))
            grid = [t[:].rearrange("p (m j) -> p m j", j=FINE) for t in (cos, cos_t)]
            v.tensor_tensor(grid[0], cc, fc, ALU.mult)
            link(v.tensor_tensor(grid[1], cs, fs, ALU.mult))
            link(v.tensor_tensor(cos[:], cos[:], cos_t[:], ALU.subtract))
            v.wait_ge(cst, 9)
            link(v.tensor_scalar(carry[:], swap[:], coarse[:, 1, COARSE:COARSE + 1], None, ALU.mult))
            v.wait_ge(ld_c, 32)
            v.scalar_tensor_tensor(carry[:], ident[:], coarse[:, 0, COARSE:COARSE + 1], carry[:],
                                   ALU.mult, ALU.add).then_inc(tabled, 1)
            v.tensor_scalar(cw[:, 0, :], ct_s[:, 0, :], sign[:], None, ALU.mult).then_inc(tabled, 1)
            v.tensor_scalar(cw[:, 1, :], ct_s[:, 1, :], -1.0, None, ALU.mult).then_inc(tabled, 1)

            def turn(g):
                v.wait_ge(bu_done, 2 * g + 1)
                if g == 0:
                    v.wait_ge(powed, 4)
                    link(v.tensor_tensor(pw[:, 4:5], pw[:, 3:4], sign[:], ALU.mult))
                v.scalar_tensor_tensor(t1[:, g, :], HB[0][:], pw[:, 3:4], cos[:], ALU.mult, ALU.mult).then_inc(turned, 1)
                v.wait_ge(bu_done, 2 * g + 2)
                if g == 0:
                    v.wait_ge(sin_made, 3)
                v.scalar_tensor_tensor(t2[:, g, :], HB[1][:], pw[:, 4:5], sin[:], ALU.mult, ALU.mult).then_inc(turned, 1)

            def scan(g):
                v.wait_ge(v_made, g + 1)
                start = 0.0
                if g % SEQ_GROUPS:
                    v.wait_ge(carried, g // SEQ_GROUPS + 1)
                    start = LB[:, GT - 1:GT]
                v.tensor_tensor_scan(zs[:, g, :], pw[:, 2:3].broadcast_to([P, GT]), t1[:, g, :], start,
                                     ALU.mult, ALU.add).then_inc(scanned, 1)
                v.wait_ge(scanned, g + 1)
                v.tensor_tensor(t1[:, g, :], cos[:], zs[:, g, :], ALU.mult).then_inc(u1_made, 1)

            for k in range(GROUPS + 2):
                if 1 <= k < GROUPS:
                    v.wait_ge(ld_x[k], 16)
                    stats(0, k, xs, stats1)
                if 1 <= k <= GROUPS:
                    turn(k - 1)
                if 1 <= k < GROUPS:
                    offset(0, k, rstd1, nmr1)
                if k >= 2:
                    g = k - 2
                    v.wait_ge(y_done, g + 1)
                    v.tensor_tensor(x1[:, tiles(g), :], xs[:, tiles(g), :],
                                    YF[g % 2][:].rearrange("p (i c) -> p i c", c=C), ALU.add).then_inc(x1_made, 1)
                    v.wait_ge(x1_made, g + 1)
                    stats(1, g, x1, stats2)
                if 1 <= k <= GROUPS:
                    scan(k - 1)
                if k >= 2:
                    offset(1, k - 2, rstd2, nmr2)

            wide = [P, TILES, E]
            v.wait_ge(lg_done, GROUPS)
            lgp = LB[:, 0:TILES * E].rearrange("p (i e) -> p i e", e=E)
            link(v.tensor_reduce(lmax[:], lgp, AX.X, ALU.max))
            v.tensor_tensor(lg[:], lgp, lmax[:, :, None].broadcast_to(wide), ALU.subtract).then_inc(lmaxed, 1)
            v.wait_ge(exped, 1)
            link(v.tensor_reduce(gsum[:], gates[:], AX.X, ALU.add))
            link(v.reciprocal(ginv[:], gsum[:]))
            link(v.tensor_tensor(gates[:], gates[:], ginv[:, :, None].broadcast_to(wide), ALU.mult))
            v.wait_ge(cst, CONSTS)
            left = gates
            for k in range(K):
                link(v.tensor_reduce(top[:, k, :], left[:], AX.X, ALU.max))
                link(v.tensor_tensor(pick[:], left[:], top[:, k, :, None].broadcast_to(wide), ALU.is_equal))
                link(v.tensor_tensor(pick[:], pick[:], rank_iota[:, None, :].broadcast_to(wide), ALU.mult))
                link(v.tensor_reduce(key[:], pick[:], AX.X, ALU.max))
                ins = v.tensor_tensor(chosen[:, k, :, :], pick[:], key[:, :, None].broadcast_to(wide), ALU.is_equal)
                if k == 0:
                    link(ins)
                    link(v.scalar_tensor_tensor(rest[:], chosen[:, 0, :, :], -2.0, gates[:], ALU.mult, ALU.add))
                    left = rest
                else:
                    ins.then_inc(routed, 1)
            v.tensor_tensor(wtmp[:, 0, :], top[:, 1, :], top[:, 0, :], ALU.subtract).then_inc(wexp, 1)
            v.wait_ge(exped, 2)
            link(v.tensor_scalar(wtmp[:, 2, :], wtmp[:, 1, :], 1.0, None, ALU.add))
            link(v.reciprocal(wk[:, 0, :], wtmp[:, 2, :]))
            link(v.tensor_tensor(wk[:, 1, :], wk[:, 0, :], wtmp[:, 1, :], ALU.mult))

            v.wait_ge(prefixed, 2)
            ps, tot = (YF[1][:, n * 256:n * 256 + 256] for n in (0, 1))
            link(v.tensor_tensor_scan(upto[:].rearrange("p e j -> p (e j)"), restart[:].rearrange("p e j -> p (e j)"),
                                      tot, 0.0, ALU.mult, ALU.add))
            link(v.tensor_tensor(full[:], upto[:, :, BLOCKS - 1:BLOCKS].broadcast_to([P, E, 16]),
                                 step_iota[:, None, :].broadcast_to([P, E, 16]), ALU.is_gt))
            link(v.tensor_reduce(units[:], full[:], AX.X, ALU.add))
            link(v.tensor_tensor_scan(units_to[:], ones[:, 0:E], units[:], 0.0, ALU.mult, ALU.add))
            link(v.tensor_tensor(first[:], units_to[:], units[:], ALU.subtract))
            v.tensor_tensor(posn[:], upto[:], tot.rearrange("p (e j) -> p e j", e=E), ALU.subtract)
            link(v.tensor_scalar(first[:], first[:], float(P), None, ALU.mult))
            link(v.tensor_tensor(posn[:], posn[:], first[:, :, None].broadcast_to([P, E, BLOCKS]), ALU.add))
            link(v.tensor_tensor(posn[:], posn[:], ps.rearrange("p (e j) -> p e j", e=E), ALU.add))
            link(v.tensor_tensor(posn[:], posn[:], chosen[:].rearrange("p k i e -> p e (k i)"), ALU.mult))
            link(v.tensor_reduce(pos[:], posn[:].rearrange("p e j -> p j e"), AX.X, ALU.add))
            link(v.tensor_copy(pos_i[:], pos[:]))
            v.tensor_scalar(pu_i[:], pos_i[:], 7, None, ALU.logical_shift_right)
            link(v.tensor_scalar(pr_i[:], pos_i[:], P - 1, None, ALU.bitwise_and))
            v.tensor_copy(pu[:], pu_i[:])
            link(v.tensor_copy(pr[:], pr_i[:]))
            per_unit = [P, BLOCKS, UNITS]
            v.tensor_tensor(in_unit[:], pu[:, :, None].broadcast_to(per_unit),
                            unit_iota[:, None, 0:UNITS].broadcast_to(per_unit), ALU.is_equal).then_inc(rows_made, 1)
            v.wait_ge(rows_made, 1)
            v.tensor_scalar(from_who[:, :, 0, :], in_unit[:], part_iota[:], None, ALU.mult)
            for q in range(4):
                part = slice(q * BLOCKS // 4, (q + 1) * BLOCKS // 4)
                per_row = [P, BLOCKS // 4, P]
                v.tensor_tensor(in_row[:, part, :], pr[:, part, None].broadcast_to(per_row),
                                row_iota[:, None, :].broadcast_to(per_row), ALU.is_equal).then_inc(posed, 1)
            every = [1, UNITS + 2, E]
            link(v.tensor_tensor(past[:], units_to[0:1, None, :].broadcast_to(every),
                                 unit_iota[0:1, :, None].broadcast_to(every), ALU.is_le))
            link(v.tensor_reduce(who[:], past[:], AX.X, ALU.add))
            link(v.tensor_scalar(who[:], who[:], float(E - 1), float(WCOLS), ALU.min, ALU.mult))
            v.tensor_copy(who0_i[:, 0:2], who[:, 0:2])
            v.tensor_copy(who_i[:].rearrange("o (n q) -> o n q", q=4)[:, :, 0:RING],
                          who[:, 2:].rearrange("o (n q) -> o n q", q=RING)).then_inc(who_made, 1)

            def add_shared(g):
                v.wait_ge(sh2, g + 1)
                v.wait_ge(acc_made, g + 1)
                v.tensor_tensor(acc[:, tiles(g), :], acc[:, tiles(g), :],
                                YF[0][:].rearrange("p (i c) -> p i c", c=C), ALU.add).then_inc(sh_added, 1)

            add_shared(0)
            v.wait_ge(inv_done, 1)
            link(v.tensor_copy(inv[:].rearrange("p n u -> p (n u)"), LB[:, P:P + 2 * UNITS]))
            v.scalar_tensor_tensor(spare[:], inv[:, 1, :], 0.0, spare_iota[:], ALU.is_equal, ALU.mult)
            link(v.scalar_tensor_tensor(dest[:], inv[:, 1, :], float(P), inv[:, 0, :], ALU.mult, ALU.add))
            link(v.scalar_tensor_tensor(dest[:], dest[:], -float(P), spare[:], ALU.add, ALU.add))
            v.tensor_copy(dest_u[:], dest[:]).then_inc(idx_made, 1)
            v.wait_ge(idx_made, 1)
            v.tensor_scalar(tok_u[:], dest_u[:], TOKENS - 1, None, ALU.bitwise_and).then_inc(idx_made, 1)

            def set_weights(off, b):
                v.tensor_copy(wring[:, b, :], exw_s[:, bass.ds(off, WCOLS)]).then_inc(w_set, 1)

            def take_x(u, b):
                v.wait_ge(turned_x, u + 1)
                v.tensor_copy(xgt[:, b, :], TB[:, 0:P]).then_inc(xgt_made, 1)

            def offsets(regs, src):
                v.load(regs, src)
                return [v.snap(r, min_val=0, max_val=(E - 1) * WCOLS) for r in regs]

            def take_y(it, b):
                u = it * RING + b
                v.wait_ge(s2_done, u + 1)
                if not (isinstance(it, int) and it == 0):
                    v.wait_ge(scattered[b], it * 16)
                v.tensor_tensor(ys[:, b, :], YB[:, 0:C], wring[:, b, OB2:], ALU.add).then_inc(ys_made, 1)

            def unit(it, b, offs, begin=False, end=False):
                u = it * RING + b
                if not (end and b == RING - 1):
                    take_x(u + 1, (b + 1) % RING)
                if not (begin and b == 0):
                    take_y(it if b else it - 1, (b - 1) % RING)
                if not (end and b > 0):
                    if not (begin and b == 0):
                        v.wait_ge(ys_made, u)
                    set_weights(offs[b], (b + 2) % RING)

            regs = [v.alloc_register(f"offset{n}") for n in range(RING)]
            v.wait_ge(ld_ex, 32)
            v.wait_ge(who_made, 1)
            for b, off in enumerate(offsets(regs[0:2], who0_i[0:1, 0:2])):
                set_weights(off, b)
            add_shared(1)
            add_shared(2)
            take_x(0, 0)
            add_shared(3)
            offs = offsets(regs, who_i[0:1, 0:RING])
            for b in range(RING):
                unit(0, b, offs, begin=True)
            with v.Fori(1, ROUNDS - 1) as it:
                offs = offsets(regs, who_i[0:1, bass.ds(it * 4, RING)])
                for b in range(RING):
                    unit(it, b, offs)
            offs = offsets(regs[0:1], who_i[0:1, 4 * (ROUNDS - 1):4 * (ROUNDS - 1) + 1])
            for b in range(RING):
                unit(ROUNDS - 1, b, offs, end=True)
            take_y(ROUNDS - 1, RING - 1)

            for g in range(GROUPS):
                v.wait_ge(ld_y[g], 32)
                for k in range(K):
                    for i in range(TG * g, TG * g + TG):
                        ins = v.scalar_tensor_tensor(acc[:, i, :], yk[k][:, i, :], wk[:, k, i:i + 1], acc[:, i, :],
                                                     ALU.mult, ALU.add)
                        if k == K - 1:
                            ins.then_inc(summed, 1)
                    if k == 0:
                        link(v.tensor_copy(coarse_done[:], wk[:, 0, 0:1]))

        @block.tensor
        def _(pe):
            def transposes(dst, src, g, ready, signal):
                pe.wait_ge(ready, TG * (g + 1))
                for i in range(TG):
                    ins = pe.transpose(dst[:, i * P:i * P + P], src[:, TG * g + i, :], ident[:])
                ins.then_inc(signal, 1)

            def inputs(g):
                pe.wait_ge(xnt_made, g + 1)
                for n in range(2):
                    if g:
                        pe.wait_ge(turned, 2 * (g - 1) + n + 1)
                    pe.matmul(HB[n][:], bt_s[:, n, :], xnt[:, toks(g)], start=True, stop=True).then_inc(bu_done, 1)

            def outputs(g):
                if g >= 2:
                    pe.wait_ge(x1_made, g - 1)
                pe.wait_ge(u1_made, g + 1)
                pe.wait_ge(u2_made, g + 1)
                for i in range(TG):
                    tok = slice(i * P, i * P + P)
                    o = YF[g % 2][:, i * C:i * C + C]
                    pe.matmul(o, xnt[:, GT * g + i * P:GT * g + i * P + P], dt_s[:], start=True, stop=False)
                    pe.matmul(o, t1[:, g, tok], cw[:, 0, :], start=False, stop=False)
                    ins = pe.matmul(o, t2[:, g, tok], cw[:, 1, :], start=False, stop=True)
                ins.then_inc(y_done, 1)

            def logits(g):
                pe.wait_ge(xn2t_made, g + 1)
                if g:
                    pe.wait_ge(h1_made, g)
                pe.matmul(HB[2][0:R, :], wr1_s[:], xn2t[:, toks(g)], start=True, stop=True).then_inc(h1_done, 1)
                pe.wait_ge(h1_made, g + 1)
                for i in range(TG * g, TG * g + TG):
                    ins = pe.matmul(LB[:, i * E:i * E + E], h1[:, i * P:i * P + P], wr2_s[:], start=True, stop=True)
                ins.then_inc(lg_done, 1)

            pe.wait_ge(cst, 6)
            for k in range(GROUPS + 2):
                if 1 <= k <= GROUPS:
                    if k == 1:
                        pe.wait_ge(ld_b, 16)
                    inputs(k - 1)
                if k < GROUPS:
                    if k:
                        pe.wait_ge(xnt_made, k)
                    transposes(TB, xn, k, xn1_made, t1_done)
                if k >= 2:
                    if k == 2:
                        pe.wait_ge(ld_c, 32)
                        pe.wait_ge(tabled, 4)
                    outputs(k - 2)
                if 1 <= k <= GROUPS and (k - 1) % SEQ_GROUPS == 0:
                    if k == 1:
                        pe.wait_ge(tabled, 2)
                    pe.wait_ge(scanned, k)
                    pe.matmul(LB[:, GT - 1:GT], carry[:], zs[:, k - 1, GT - 1:GT], start=True, stop=True).then_inc(carried, 1)
                if k >= 2:
                    g = k - 2
                    if g:
                        pe.wait_ge(xn2t_made, g)
                    transposes(YB, xn, g, xn2_made, t2_done)
                    if g == 0:
                        pe.wait_ge(ld_r, 48)
                    logits(g)

            def shared_1(g):
                for c in range(IC):
                    n = g * IC + c
                    if n == 0:
                        pe.wait_ge(ld_sh, 32)
                        pe.wait_ge(turned, 2 * GROUPS)
                    if n >= 3:
                        pe.wait_ge(sh_act, n - 2)
                    pe.matmul(HB[n % 3][:], shw_s[:, c * P:c * P + P], xn2t[:, toks(g)],
                              start=True, stop=True).then_inc(sh1, 1)

            def shared_2(g):
                pe.wait_ge(sh_act, IC * (g + 1))
                if g:
                    pe.wait_ge(sh_added, g)
                else:
                    pe.wait_ge(x1_made, GROUPS)
                for i in range(TG):
                    for c in range(IC):
                        ins = pe.matmul(YF[0][:, i * C:i * C + C], hs[:, g % 2, c, i * P:i * P + P],
                                        shw_s[:, OW2 + c * C:OW2 + c * C + C], start=(c == 0), stop=(c == IC - 1))
                ins.then_inc(sh2, 1)

            shared_1(0)
            pe.wait_ge(cst, CONSTS)
            pe.wait_ge(routed, 1)
            rows = chosen[:].rearrange("p k i e -> p e (k i)")
            for n, lhs in enumerate((before, ones)):
                pe.matmul(YF[1][:, n * 256:n * 256 + 256], lhs[:], rows, start=True, stop=True).then_inc(prefixed, 1)
            shared_1(1)
            shared_2(0)
            pe.wait_ge(blocks_made, 1)
            pe.wait_ge(posed, 4)
            for j in range(BLOCKS):
                ins = pe.matmul(LB[:, P:P + 2 * UNITS], in_row[:, j, :], from_who[:, j, :, :].rearrange("p n u -> p (n u)"),
                                start=(j == 0), stop=(j == BLOCKS - 1))
            ins.then_inc(inv_done, 1)
            shared_1(2)
            shared_2(1)
            shared_1(3)
            shared_2(2)

            def turn_x(it, b):
                pe.wait_ge(gathered[b], it * 16 + 16)
                if isinstance(it, int) and it * RING + b == 0:
                    pe.wait_ge(xnt_made, GROUPS)
                else:
                    pe.wait_ge(xgt_made, it * RING + b)
                pe.transpose(TB[:, 0:P], xg[:, b, :], ident[:]).then_inc(turned_x, 1)

            def up(it, b):
                u = it * RING + b
                if isinstance(it, int) and u == 0:
                    pe.wait_ge(sh_act, IC * GROUPS)
                    pe.wait_ge(sh_added, GROUPS)
                pe.wait_ge(w_set, u + 1)
                pe.wait_ge(xgt_made, u + 1)
                for c in range(IC):
                    ins = pe.matmul(HU[b][c // 2][:, c % 2 * P:c % 2 * P + P], wring[:, b, c * P:c * P + P],
                                    xgt[:, b, :], start=True, stop=True)
                    if c % 2:
                        ins.then_inc(s1_done, 1)

            def down(it, b):
                u = it * RING + b
                if isinstance(it, int) and u == 0:
                    pe.wait_ge(xn2t_made, GROUPS)
                else:
                    pe.wait_ge(ys_made, u)
                for c in range(IC):
                    pe.wait_ge(h_made, u * IC + c + 1)
                    ins = pe.matmul(YB[:, 0:C], he[:, b, c, :], wring[:, b, OW2 + c * C:OW2 + c * C + C],
                                    start=(c == 0), stop=(c == IC - 1))
                ins.then_inc(s2_done, 1)

            def unit(it, b, begin=False, end=False):
                if not (end and b == RING - 1):
                    turn_x(it + (b + 1) // RING, (b + 1) % RING)
                up(it, b)
                if not (begin and b == 0):
                    down(it if b else it - 1, (b - 1) % RING)

            turn_x(0, 0)
            shared_2(3)
            for b in range(RING):
                unit(0, b, begin=True)
            with pe.Fori(1, ROUNDS - 1) as it:
                for b in range(RING):
                    unit(it, b)
            for b in range(RING):
                unit(ROUNDS - 1, b, end=True)
            down(ROUNDS - 1, RING - 1)


def kernel(**inputs):
    import numpy as np
    import concourse.bacc as bacc
    from concourse.bass_utils import run_bass_kernel_spmd

    a = {name.replace("L0_", ""): np.asarray(value) for name, value in inputs.items()}

    def down(w):
        return w.reshape(IC, P, C).transpose(1, 0, 2).reshape(P, IC * C)

    arrays = {
        "x": a["attn_x"],
        "prm": np.tile(np.stack([a["attn_nu_log"], a["attn_theta_log"], a["attn_gamma_log"]], 1), (2, 1)),
        "bt": np.stack([np.concatenate([a["attn_B_re"], a["attn_B_im"]]).T,
                        np.concatenate([a["attn_B_im"], a["attn_B_re"]]).T], 1),
        "ct": np.stack([np.concatenate([a["attn_C_re"], a["attn_C_im"]], 1).T,
                        np.concatenate([a["attn_C_im"], a["attn_C_re"]], 1).T], 1),
        "dt": a["attn_D"].T,
        "wr1": a["ffn_Wr1"],
        "br1": a["ffn_br1"][:, None],
        "wr2": np.concatenate([a["ffn_Wr2"], a["ffn_br2"][None]]),
        "shw": np.concatenate([a["ffn_Ws1"], down(a["ffn_Ws2"]), a["ffn_bs1"].reshape(IC, P).T], 1),
        "bs2": a["ffn_bs2"][None],
        "exw": np.stack([np.concatenate([a["ffn_We1"][e], down(a["ffn_We2"][e]), a["ffn_be1"][e].reshape(IC, P).T], 1)
                         for e in range(E)], 1),
        "be2": a["ffn_be2"][None],
    }
    nc = bacc.Bacc("TRN2", target_bir_lowering=False, num_devices=1)
    feeds, aps = {}, []
    for name, value in arrays.items():
        feeds[f"in_{name}"] = np.ascontiguousarray(value)
        aps.append(nc.dram_tensor(f"in_{name}", value.shape, mybir.dt.from_np(value.dtype), kind="ExternalInput").ap())
    shape = a["attn_x"].shape
    aps.append(nc.dram_tensor("out_x", shape, F32, kind="ExternalOutput").ap())
    seq_moe_kernel(nc, *aps)
    r = run_bass_kernel_spmd(nc, [feeds], core_ids=[0])
    return r.results[0]["out_x"]
```

```python
from contextlib import ExitStack

import concourse.bass as bass
from concourse import mybir

F32 = mybir.dt.float32
BF16 = mybir.dt.bfloat16
I32 = mybir.dt.int32
U32 = mybir.dt.uint32
ALU = mybir.AluOpType
ACT = mybir.ActivationFunctionType
AX = mybir.AxisListType

P = 128
TILES = 16
GROUPS = 4
TG = TILES // GROUPS
GT = TG * P
SEQ_GROUPS = 2
NS = 64
C = 128
I = 512
IC = I // P
E = 8
K = 2
R = 32
TOKENS = TILES * P
BLOCKS = K * TILES
UNITS = K * TOKENS // P + E - 1
RING = 3
AHEAD = 6
ROUND = 6
ROUNDS = UNITS // ROUND
FINE = 32
COARSE = GT // FINE
OW2, OB1, OB2, WCOLS = I, 2 * I, 2 * I + IC, 2 * I + IC + C
EPS = 1e-5
TO_INT = 12582912.0
TWO_PI_HI, TWO_PI_LO = 6.28125, 0.0019353071795864769
PI_DOWN = 3.1415925
assert ROUND % RING == 0 and ROUND % AHEAD == 0 and UNITS % RING == 0


def seq_moe_kernel(nc, x, prm, bt, ct, dt, wr1, br1, wr2, br2, shw, bs2, exw, be2, out):
    xn_dram = nc.dram_tensor("xn_rows", [TOKENS, C], F32, kind="Internal").ap()
    y_dram = nc.dram_tensor("y_rows", [K * TOKENS + UNITS * P, C], F32, kind="Internal").ap()

    with ExitStack() as ctx:
        def sb(name, shape, dtype=F32):
            return ctx.enter_context(nc.sbuf_tensor(name, shape, dtype))

        def sem(name):
            return ctx.enter_context(nc.semaphore(name))

        ident = sb("ident", [P, P])
        before = sb("before", [P, P], BF16)
        ones = sb("ones", [P, P], BF16)
        swap = sb("swap", [P, P])
        row_iota = sb("row_iota", [P, P])
        unit_iota = sb("unit_iota", [P, UNITS + 2])
        block_iota = sb("block_iota", [P, BLOCKS])
        part_iota = sb("part_iota", [P, 1])
        step_iota = sb("step_iota", [P, TOKENS // P])
        spare_iota = sb("spare_iota", [P, UNITS])
        rank_iota = sb("rank_iota", [P, E])
        restart = sb("restart", [P, E, BLOCKS])
        euler = sb("euler", [P, 1])
        inv_euler = sb("inv_euler", [P, 1])
        neg_half = sb("neg_half", [P, TG])
        sign = sb("sign", [P, 1])
        half_pi = sb("half_pi", [P, 1])
        prm_s = sb("prm_s", [P, 3])
        bt_s = sb("bt_s", [P, 2, P])
        ct_s = sb("ct_s", [P, 2, C])
        cw = sb("cw", [P, 2, C])
        dt_s = sb("dt_s", [P, C])
        wr1_s = sb("wr1_s", [P, R])
        br1_s = sb("br1_s", [R, 1])
        wr2_s = sb("wr2_s", [R, E])
        br2_s = sb("br2_s", [P, E])
        shw_s = sb("shw_s", [P, OB2])
        bs2_s = sb("bs2_s", [P, C])
        exw_s = sb("exw_s", [P, E * WCOLS])
        pw = sb("pw", [P, 5])
        ang = sb("ang", [P, 8])
        steps = sb("steps", [P, FINE + COARSE + 1])
        angs = sb("angs", [P, 4, FINE + COARSE + 1])
        turns = sb("turns", [P, 2, FINE + COARSE + 1])
        pause = sb("pause", [P, 1])
        cos = sb("cos", [P, GT])
        sin = sb("sin", [P, GT])
        cos_t = sb("cos_t", [P, GT])
        sin_t = sb("sin_t", [P, GT])
        carry = sb("carry", [P, P])
        fine, coarse = turns[:, :, 0:FINE], turns[:, :, FINE:]
        xs = sb("xs", [P, TILES, C])
        xn = sb("xn", [P, TILES, C])
        xnt = sb("xnt", [P, TOKENS])
        x1 = sb("x1", [P, TILES, C])
        acc = sb("acc", [P, TILES, C])
        xn2t = sb("xn2t", [P, TOKENS])
        bn = sb("bn", [P, 2, TILES, 6])
        mv = sb("mv", [P, 2, TILES, 2])
        veps = sb("veps", [P, 2, TILES])
        rstd = sb("rstd", [P, 2, TILES])
        nmr = sb("nmr", [P, 2, TILES])
        t1 = sb("t1", [P, GROUPS, GT])
        t2 = sb("t2", [P, GROUPS, GT])
        zs = sb("zs", [P, GROUPS, GT])
        h1 = sb("h1", [R, TOKENS])
        lg = sb("lg", [P, TILES, E])
        lmax = sb("lmax", [P, TILES])
        gates = sb("gates", [P, TILES, E])
        rest = sb("rest", [P, TILES, E])
        pick = sb("pick", [P, TILES, E])
        gsum = sb("gsum", [P, TILES])
        ginv = sb("ginv", [P, TILES])
        top = sb("top", [P, K, TILES])
        key = sb("key", [P, TILES])
        wk = sb("wk", [P, K, TILES])
        wtmp = sb("wtmp", [P, 3, TILES])
        chosen = sb("chosen", [P, K, TILES, E], BF16)
        upto = sb("upto", [P, E, BLOCKS])
        posn = sb("posn", [P, E, BLOCKS])
        full = sb("full", [P, E, 16])
        units = sb("units", [P, E])
        units_to = sb("units_to", [P, E])
        first = sb("first", [P, E])
        pos = sb("pos", [P, BLOCKS])
        pos_i = sb("pos_i", [P, BLOCKS], I32)
        pu_i = sb("pu_i", [P, BLOCKS], I32)
        pr_i = sb("pr_i", [P, BLOCKS], I32)
        pu = sb("pu", [P, BLOCKS])
        pr = sb("pr", [P, BLOCKS])
        in_row = sb("in_row", [P, BLOCKS, P], BF16)
        in_unit = sb("in_unit", [P, BLOCKS, UNITS], BF16)
        from_who = sb("from_who", [P, BLOCKS, 2, UNITS], BF16)
        inv = sb("inv", [P, 2, UNITS])
        spare = sb("spare", [P, UNITS])
        dest = sb("dest", [P, UNITS])
        dest_u = sb("dest_u", [P, UNITS], U32)
        tok_u = sb("tok_u", [P, UNITS], U32)
        past = sb("past", [1, UNITS + 2, E])
        who = sb("who", [1, UNITS + 2])
        who_i = sb("who_i", [1, ROUND * (ROUNDS + 1) + 2], I32)
        hs = sb("hs", [P, 2, IC, GT])
        wring = sb("wring", [P, RING, WCOLS])
        xg = sb("xg", [P, AHEAD, C])
        xgt = sb("xgt", [P, RING, P])
        he = sb("he", [P, RING, IC, P])
        ys = sb("ys", [P, RING, C])
        yk = [t[:].rearrange("p g (i c) -> p (g i) c", c=C) for t in (t1, t2)]

        bank = [ctx.enter_context(nc.psum_tensor(f"bank{i}", [P, GT], F32)) for i in range(8)]
        HB = bank[0:3]
        HU = [(bank[0], bank[7]), (bank[1], bank[6]), (bank[2], bank[5])]
        TB, YB = bank[3], bank[4]
        YF = bank[5:7]
        LB = bank[7]

        ld_x = [sem(f"ld_x{g}") for g in range(GROUPS)]
        ld_prm, ld_b, ld_c, ld_r, ld_sh, ld_ex = (sem(n) for n in ("ld_prm", "ld_b", "ld_c", "ld_r", "ld_sh", "ld_ex"))
        cst, powed, sined, angled, tabled, sin_made = (sem(n) for n in ("cst", "powed", "sined", "angled", "tabled", "sin_made"))
        stats1, rstd1, nmr1, xn1_made, t1_done, xnt_made = (sem(n) for n in ("stats1", "rstd1", "nmr1", "xn1_made", "t1_done", "xnt_made"))
        bu_done, turned, v_made, scanned, u1_made, u2_made, carried = (sem(n) for n in ("bu_done", "turned", "v_made", "scanned", "u1_made", "u2_made", "carried"))
        y_done, x1_made, stats2, rstd2, nmr2, xn2_made, t2_done, xn2t_made = (sem(n) for n in ("y_done", "x1_made", "stats2", "rstd2", "nmr2", "xn2_made", "t2_done", "xn2t_made"))
        acc_made, h1_done, h1_made, lg_done, xn_stored = (sem(n) for n in ("acc_made", "h1_done", "h1_made", "lg_done", "xn_stored"))
        dve, lmaxed, exped, wexp, routed, prefixed, posed, who_made, rows_made, inv_done, idx_made = (
            sem(n) for n in ("dve", "lmaxed", "exped", "wexp", "routed", "prefixed", "posed", "who_made", "rows_made", "inv_done", "idx_made"))
        blocks_made = sem("blocks_made")
        sh1, sh_act, sh2, sh_added = (sem(n) for n in ("sh1", "sh_act", "sh2", "sh_added"))
        gathered = [sem(f"gathered{b}") for b in range(AHEAD)]
        scattered = [sem(f"scattered{b}") for b in range(RING)]
        turned_x, xgt_made, s1_done, h_made, s2_done, ys_made, w_set = (
            sem(n) for n in ("turned_x", "xgt_made", "s1_done", "h_made", "s2_done", "ys_made", "w_set"))
        ld_y = [sem(f"ld_y{g}") for g in range(GROUPS)]
        summed, stored = sem("summed"), sem("stored")

        CONSTS = 22
        y_view = y_dram[0:K * TOKENS, :].rearrange("(k i p) c -> p k i c", k=K, p=P)
        x_view = x.rearrange("b (i p) c -> p (b i) c", p=P)
        out_view = out.rearrange("b (i p) c -> p (b i) c", p=P)
        xn_view = xn_dram.rearrange("(i p) c -> p i c", p=P)

        def tiles(g):
            return slice(TG * g, TG * g + TG)

        def toks(g):
            return slice(GT * g, GT * g + GT)

        block = ctx.enter_context(nc.Block())

        @block.sync
        def _(sp):
            sp.dma_start(prm_s[:], prm).then_inc(ld_prm, 16)
            for g in range(GROUPS):
                sp.dma_start(xs[:, tiles(g), :], x_view[:, tiles(g), :]).then_inc(ld_x[g], 16)
                if g == 0:
                    sp.dma_start(bt_s[:], bt).then_inc(ld_b, 16)
            sp.dma_start(ct_s[:], ct).then_inc(ld_c, 16)
            sp.dma_start(dt_s[:], dt).then_inc(ld_c, 16)
            sp.dma_start(wr1_s[:], wr1).then_inc(ld_r, 16)
            sp.dma_start(br1_s[:], br1).then_inc(ld_r, 16)
            sp.dma_start(wr2_s[:], wr2).then_inc(ld_r, 16)
            sp.dma_start(br2_s[:], br2.broadcast_to([P, E])).then_inc(ld_r, 16)
            sp.dma_start(bs2_s[:], bs2.broadcast_to([P, C])).then_inc(ld_sh, 16)
            sp.dma_start(shw_s[:], shw).then_inc(ld_sh, 16)
            ex = exw_s[:].rearrange("p (e w) -> p e w", e=E)
            sp.dma_start(ex[:, :, OB2:], be2.broadcast_to([P, E, C])).then_inc(ld_ex, 16)
            sp.dma_start(ex[:, :, 0:OB2], exw).then_inc(ld_ex, 16)
            for g in range(GROUPS):
                sp.wait_ge(xn2_made, TG * (g + 1))
                sp.dma_start(xn_view[:, tiles(g), :], xn[:, tiles(g), :]).then_inc(xn_stored, 16)
            for b in range(RING):
                sp.wait_ge(scattered[b], 16 * (UNITS // RING))
            for g in range(GROUPS):
                for k in range(K):
                    sp.dma_start(yk[k][:, tiles(g), :], y_view[:, k, tiles(g), :]).then_inc(ld_y[g], 16)
            for g in range(GROUPS):
                sp.wait_ge(summed, TG * (g + 1))
                sp.dma_start(out_view[:, tiles(g), :], acc[:, tiles(g), :]).then_inc(stored, 16)
            sp.wait_ge(stored, 16 * GROUPS)
            sp.wait_ge(xn_stored, 16 * GROUPS)

        @block.gpsimd
        def _(pool):
            pool.memset(euler[:], 2.718281828459045).then_inc(cst, 1)
            pool.memset(inv_euler[:], 0.36787944117144233).then_inc(cst, 1)
            pool.memset(neg_half[:], -0.5).then_inc(cst, 1)
            pool.memset(half_pi[:], 1.5707963267948966).then_inc(cst, 1)
            pool.iota(steps[:, 0:FINE], [[1, FINE]], base=1, channel_multiplier=0,
                      allow_small_or_imprecise_dtypes=True).then_inc(cst, 1)
            pool.iota(steps[:, FINE:], [[FINE, COARSE + 1]], base=0, channel_multiplier=0,
                      allow_small_or_imprecise_dtypes=True).then_inc(cst, 1)
            pool.wait_ge(ld_prm, 16)
            pool.wait_ge(cst, 4)
            pool.tensor_tensor(pw[:, 0:1], euler[:], prm_s[:, 1:2], ALU.pow).then_inc(powed, 1)
            pool.tensor_tensor(pw[:, 1:2], euler[:], prm_s[:, 0:1], ALU.pow).then_inc(powed, 1)
            pool.tensor_tensor(pw[:, 3:4], euler[:], prm_s[:, 2:3], ALU.pow).then_inc(powed, 1)
            pool.wait_ge(powed, 3)
            pool.tensor_tensor(pw[:, 2:3], inv_euler[:], pw[:, 1:2], ALU.pow).then_inc(powed, 1)
            pool.memset(ident[:], 0.0).then_inc(cst, 1)
            pool.wait_ge(cst, 7)
            pool.affine_select(out=ident[:], in_=ident[:], compare_op=ALU.not_equal, fill=1.0, base=0,
                               pattern=[[-1, P]], channel_multiplier=1).then_inc(cst, 1)

            def rstd_of(n, g, signal, ready):
                pool.wait_ge(ready, g + 1)
                pool.tensor_tensor(rstd[:, n, tiles(g)], veps[:, n, tiles(g)], neg_half[:], ALU.pow).then_inc(signal, 1)

            def add_v(g):
                pool.wait_ge(turned, 2 * (g + 1))
                pool.tensor_tensor(t1[:, g, :], t1[:, g, :], t2[:, g, :], ALU.add).then_inc(v_made, 1)

            def turn_back(g):
                pool.wait_ge(scanned, g + 1)
                pool.tensor_tensor(t2[:, g, :], sin[:], zs[:, g, :], ALU.mult).then_inc(u2_made, 1)

            def start_acc(g):
                if g == 0:
                    pool.wait_ge(ld_sh, 32)
                pool.wait_ge(x1_made, g + 1)
                pool.tensor_tensor(acc[:, tiles(g), :], x1[:, tiles(g), :],
                                   bs2_s[:, None, :].broadcast_to([P, TG, C]), ALU.add).then_inc(acc_made, 1)

            rstd_of(0, 0, rstd1, stats1)
            pool.memset(swap[:], 0.0).then_inc(cst, 1)
            pool.wait_ge(cst, 9)
            pool.affine_select(out=swap[:], in_=swap[:], compare_op=ALU.not_equal, fill=1.0, base=NS,
                               pattern=[[-1, P]], channel_multiplier=1).then_inc(cst, 1)
            pool.wait_ge(cst, 10)
            pool.affine_select(out=swap[:], in_=swap[:], compare_op=ALU.not_equal, fill=-1.0, base=-NS,
                               pattern=[[-1, P]], channel_multiplier=1).then_inc(cst, 1)
            pool.wait_ge(sined, 2)
            shape = [P, COARSE, FINE]
            cc, cs = (coarse[:, n, 0:COARSE][:, :, None].broadcast_to(shape) for n in (0, 1))
            fc, fs = (fine[:, n, None, :].broadcast_to(shape) for n in (0, 1))
            grid = [t[:].rearrange("p (m j) -> p m j", j=FINE) for t in (sin, sin_t)]
            pool.tensor_tensor(grid[0], cc, fs, ALU.mult).then_inc(sin_made, 1)
            pool.tensor_tensor(grid[1], cs, fc, ALU.mult).then_inc(sin_made, 1)
            pool.wait_ge(sin_made, 2)
            pool.tensor_tensor(sin[:], sin[:], sin_t[:], ALU.add).then_inc(sin_made, 1)
            pool.memset(ones[:], 1.0).then_inc(cst, 1)
            pool.wait_ge(cst, 12)
            pool.affine_select(out=before[:], in_=ones[:], compare_op=ALU.is_gt, fill=0.0, base=0,
                               pattern=[[1, P]], channel_multiplier=-1).then_inc(cst, 1)
            for t, n, step, base, cm in (
                (row_iota, P, 1, 0, 0), (unit_iota, UNITS + 2, 1, 0, 0), (block_iota, BLOCKS, 1, 1, 0),
                (part_iota, 1, 1, 0, 1), (step_iota, TOKENS // P, P, 0, 0),
                (spare_iota, UNITS, P, K * TOKENS + P, 1), (rank_iota, E, -1, E, 0),
            ):
                pool.iota(t[:], [[step, n]], base=base, channel_multiplier=cm,
                          allow_small_or_imprecise_dtypes=True).then_inc(cst, 1)
            pool.memset(restart[:], 1.0).then_inc(cst, 1)
            pool.wait_ge(cst, 21)
            pool.memset(restart[:, :, 0:1], 0.0).then_inc(cst, 1)
            for k in range(1, GROUPS + 2):
                if k >= 2:
                    rstd_of(1, k - 2, rstd2, stats2)
                if k < GROUPS:
                    rstd_of(0, k, rstd1, stats1)
                if k - 1 < GROUPS:
                    add_v(k - 1)
                    turn_back(k - 1)
                if k >= 2:
                    start_acc(k - 2)

            pool.wait_ge(rows_made, 1)
            pool.tensor_tensor(from_who[:, :, 1, :], in_unit[:],
                               block_iota[:, :, None].broadcast_to([P, BLOCKS, UNITS]), ALU.mult).then_inc(blocks_made, 1)

            def gather(u):
                b = u % AHEAD
                if u == 0:
                    pool.wait_ge(idx_made, 2)
                    pool.wait_ge(xn_stored, 16 * GROUPS)
                if u >= AHEAD:
                    pool.wait_ge(turned_x, u - AHEAD + 1)
                pool.indirect_dma_start(xg[:, b, :], None, xn_dram,
                                        bass.IndirectOffsetOnAxis(tok_u[:, u:u + 1], 0)).then_inc(gathered[b], 16)

            def scatter(u):
                b = u % RING
                pool.wait_ge(ys_made, u + 1)
                pool.indirect_dma_start(y_dram, bass.IndirectOffsetOnAxis(dest_u[:, u:u + 1], 0),
                                        ys[:, b, :], None).then_inc(scattered[b], 16)

            for u in range(UNITS + AHEAD):
                if u < UNITS:
                    gather(u)
                if u >= AHEAD:
                    scatter(u - AHEAD)

        @block.scalar
        def _(act):
            act.wait_ge(angled, 1)
            act.wait_ge(cst, 4)
            act.activation(turns[:, 1, :], angs[:, 2, :], ACT.Sin).then_inc(sined, 1)
            act.activation(turns[:, 0, :], angs[:, 3, :], ACT.Sin, bias=half_pi[:], scale=-1.0).then_inc(sined, 1)

            def normalize(n, g, src, ready, signal):
                act.wait_ge(ready, g + 1)
                for i in range(TG * g, TG * g + TG):
                    act.activation(xn[:, i, :], src[:, i, :], ACT.Identity, bias=nmr[:, n, i:i + 1],
                                   scale=rstd[:, n, i:i + 1]).then_inc(signal, 1)

            for k in range(GROUPS + 3):
                if k < GROUPS:
                    normalize(0, k, xs, nmr1, xn1_made)
                if 2 <= k < GROUPS + 2:
                    normalize(1, k - 2, x1, nmr2, xn2_made)
                if k >= 3:
                    g = k - 3
                    act.wait_ge(h1_done, g + 1)
                    if g == 0:
                        act.wait_ge(ld_r, 64)
                    act.activation(h1[:, toks(g)], HB[2][0:R, :], ACT.Relu, bias=br1_s[:]).then_inc(h1_made, 1)
                if k < GROUPS:
                    act.wait_ge(t1_done, k + 1)
                    act.copy(xnt[:, toks(k)], TB[:]).then_inc(xnt_made, 1)
                if 2 <= k < GROUPS + 2:
                    act.wait_ge(t2_done, k - 1)
                    act.copy(xn2t[:, toks(k - 2)], YB[:]).then_inc(xn2t_made, 1)

            act.wait_ge(lmaxed, 1)
            act.activation(gates[:], lg[:], ACT.Exp).then_inc(exped, 1)
            act.wait_ge(wexp, 1)
            act.activation(wtmp[:, 1, :], wtmp[:, 0, :], ACT.Exp, scale=0.5).then_inc(exped, 1)

            for g in range(GROUPS):
                for c in range(IC):
                    n = g * IC + c
                    act.wait_ge(sh1, n + 1)
                    if g >= 2:
                        act.wait_ge(sh2, g - 1)
                    act.activation(hs[:, g % 2, c, :], HB[n % 3][:], ACT.Silu,
                                   bias=shw_s[:, OB1 + c:OB1 + c + 1]).then_inc(sh_act, 1)

            def unit(u, n):
                b = n % RING
                for c in range(IC):
                    if c % 2 == 0:
                        act.wait_ge(s1_done, u * 2 + c // 2 + 1)
                    act.activation(he[:, b, c, :], HU[b][c // 2][:, c % 2 * P:c % 2 * P + P], ACT.Silu,
                                   bias=wring[:, b, OB1 + c:OB1 + c + 1]).then_inc(h_made, 1)

            for u in range(ROUND):
                unit(u, u)
            with act.Fori(1, ROUNDS) as r:
                for n in range(ROUND):
                    unit(r * ROUND + n, n)
            for u in range(ROUND * ROUNDS, UNITS):
                unit(u, u)

        @block.vector
        def _(v):
            links = [0]

            def link(ins):
                links[0] += 1
                ins.then_inc(dve, 1)
                v.wait_ge(dve, links[0])

            def stats(n, g, src, signal):
                for i in range(TG * g, TG * g + TG):
                    ins = v.bn_stats(bn[:, n, i, :], src[:, i, :])
                link(ins)
                for i in range(TG * g, TG * g + TG):
                    ins = v.bn_aggr(mv[:, n, i, :], bn[:, n, i, :])
                link(ins)
                v.tensor_scalar(veps[:, n, tiles(g)], mv[:, n, tiles(g), 1], EPS, None, ALU.add).then_inc(signal, 1)

            def offset(n, g, ready, signal):
                v.wait_ge(ready, g + 1)
                v.scalar_tensor_tensor(nmr[:, n, tiles(g)], mv[:, n, tiles(g), 0], -1.0, rstd[:, n, tiles(g)],
                                       ALU.mult, ALU.mult).then_inc(signal, 1)

            v.memset(sign[0:NS, :], 1.0)
            v.memset(sign[NS:P, :], -1.0)
            v.wait_ge(powed, 1)
            link(v.tensor_scalar(ang[:, 0:1].bitcast(U32), pw[:, 0:1].bitcast(U32), 0xFFFFF000, None, ALU.bitwise_and))
            v.tensor_scalar(ang[:, 2:3], pw[:, 0:1], 0.15915494309189535, None, ALU.mult)
            link(v.tensor_tensor(ang[:, 1:2], pw[:, 0:1], ang[:, 0:1], ALU.subtract))
            v.wait_ge(cst, 6)
            v.tensor_scalar(angs[:, 0, :], steps[:], ang[:, 0:1], None, ALU.mult)
            link(v.tensor_scalar(angs[:, 1, :], steps[:], ang[:, 2:3], TO_INT, ALU.mult, ALU.add))
            link(v.tensor_scalar(angs[:, 1, :], angs[:, 1, :], TO_INT, None, ALU.subtract))
            link(v.scalar_tensor_tensor(angs[:, 0, :], angs[:, 1, :], -TWO_PI_HI, angs[:, 0, :], ALU.mult, ALU.add))
            link(v.scalar_tensor_tensor(angs[:, 0, :], angs[:, 1, :], -TWO_PI_LO, angs[:, 0, :], ALU.mult, ALU.add))
            link(v.scalar_tensor_tensor(angs[:, 0, :], steps[:], ang[:, 1:2], angs[:, 0, :], ALU.mult, ALU.add))
            link(v.tensor_scalar(angs[:, 2, :], angs[:, 0, :], PI_DOWN, -PI_DOWN, ALU.min, ALU.max))
            v.scalar_tensor_tensor(angs[:, 3, :], angs[:, 2, :], -1.0, angs[:, 2, :], ALU.mult, ALU.max).then_inc(angled, 1)
            v.wait_ge(ld_x[0], 16)
            stats(0, 0, xs, stats1)
            def rotation():
                v.wait_ge(sined, 2)
                shape = [P, COARSE, FINE]
                cc, cs = (coarse[:, m, 0:COARSE][:, :, None].broadcast_to(shape) for m in (0, 1))
                fc, fs = (fine[:, m, None, :].broadcast_to(shape) for m in (0, 1))
                grid = [t[:].rearrange("p (m j) -> p m j", j=FINE) for t in (cos, cos_t)]
                v.tensor_tensor(grid[0], cc, fc, ALU.mult)
                link(v.tensor_tensor(grid[1], cs, fs, ALU.mult))
                link(v.tensor_tensor(cos[:], cos[:], cos_t[:], ALU.subtract))
                v.wait_ge(cst, 11)
                link(v.tensor_scalar(carry[:], swap[:], coarse[:, 1, COARSE:COARSE + 1], None, ALU.mult))
                v.wait_ge(ld_c, 32)
                v.scalar_tensor_tensor(carry[:], ident[:], coarse[:, 0, COARSE:COARSE + 1], carry[:],
                                       ALU.mult, ALU.add).then_inc(tabled, 1)
                v.tensor_scalar(cw[:, 0, :], ct_s[:, 0, :], sign[:], None, ALU.mult).then_inc(tabled, 1)
                v.tensor_scalar(cw[:, 1, :], ct_s[:, 1, :], -1.0, None, ALU.mult).then_inc(tabled, 1)

            def turn(g):
                v.wait_ge(bu_done, 2 * g + 1)
                if g == 0:
                    v.wait_ge(powed, 4)
                    link(v.tensor_tensor(pw[:, 4:5], pw[:, 3:4], sign[:], ALU.mult))
                v.scalar_tensor_tensor(t1[:, g, :], HB[0][:], pw[:, 3:4], cos[:], ALU.mult, ALU.mult).then_inc(turned, 1)
                v.wait_ge(bu_done, 2 * g + 2)
                if g == 0:
                    v.wait_ge(sin_made, 3)
                v.scalar_tensor_tensor(t2[:, g, :], HB[1][:], pw[:, 4:5], sin[:], ALU.mult, ALU.mult).then_inc(turned, 1)

            def scan(g):
                v.wait_ge(v_made, g + 1)
                start = 0.0
                if g % SEQ_GROUPS:
                    v.wait_ge(carried, g // SEQ_GROUPS + 1)
                    start = LB[:, GT - 1:GT]
                v.tensor_tensor_scan(zs[:, g, :], pw[:, 2:3].broadcast_to([P, GT]), t1[:, g, :], start,
                                     ALU.mult, ALU.add).then_inc(scanned, 1)
                v.wait_ge(scanned, g + 1)
                v.tensor_tensor(t1[:, g, :], cos[:], zs[:, g, :], ALU.mult).then_inc(u1_made, 1)

            for k in range(GROUPS + 2):
                if k >= 2:
                    g = k - 2
                    v.wait_ge(y_done, g + 1)
                    v.tensor_tensor(x1[:, tiles(g), :], xs[:, tiles(g), :],
                                    YF[0][:].rearrange("p (i c) -> p i c", c=C), ALU.add).then_inc(x1_made, 1)
                    v.wait_ge(x1_made, g + 1)
                    stats(1, g, x1, stats2)
                if 1 <= k < GROUPS:
                    v.wait_ge(ld_x[k], 16)
                    stats(0, k, xs, stats1)
                if 1 <= k <= GROUPS:
                    turn(k - 1)
                if k >= 2:
                    offset(1, k - 2, rstd2, nmr2)
                if 1 <= k < GROUPS:
                    offset(0, k, rstd1, nmr1)
                if 1 <= k <= GROUPS:
                    scan(k - 1)
                if k == 0:
                    offset(0, 0, rstd1, nmr1)
                    rotation()

            wide = [P, TILES, E]
            v.wait_ge(lg_done, GROUPS)
            lgp = LB[:, 0:TILES * E].rearrange("p (i e) -> p i e", e=E)
            v.wait_ge(ld_r, 64)
            link(v.tensor_tensor(lg[:], lgp, br2_s[:, None, :].broadcast_to(wide), ALU.add))
            link(v.tensor_reduce(lmax[:], lg[:], AX.X, ALU.max))
            v.tensor_tensor(lg[:], lg[:], lmax[:, :, None].broadcast_to(wide), ALU.subtract).then_inc(lmaxed, 1)
            v.wait_ge(exped, 1)
            link(v.tensor_reduce(gsum[:], gates[:], AX.X, ALU.add))
            link(v.reciprocal(ginv[:], gsum[:]))
            link(v.tensor_tensor(gates[:], gates[:], ginv[:, :, None].broadcast_to(wide), ALU.mult))
            v.wait_ge(cst, CONSTS)
            left = gates
            for k in range(K):
                link(v.tensor_reduce(top[:, k, :], left[:], AX.X, ALU.max))
                link(v.tensor_tensor(pick[:], left[:], top[:, k, :, None].broadcast_to(wide), ALU.is_equal))
                link(v.tensor_tensor(pick[:], pick[:], rank_iota[:, None, :].broadcast_to(wide), ALU.mult))
                link(v.tensor_reduce(key[:], pick[:], AX.X, ALU.max))
                ins = v.tensor_tensor(chosen[:, k, :, :], pick[:], key[:, :, None].broadcast_to(wide), ALU.is_equal)
                if k == 0:
                    link(ins)
                    link(v.scalar_tensor_tensor(rest[:], chosen[:, 0, :, :], -2.0, gates[:], ALU.mult, ALU.add))
                    left = rest
                else:
                    ins.then_inc(routed, 1)
            v.tensor_tensor(wtmp[:, 0, :], top[:, 1, :], top[:, 0, :], ALU.subtract).then_inc(wexp, 1)
            v.wait_ge(exped, 2)
            link(v.tensor_scalar(wtmp[:, 2, :], wtmp[:, 1, :], 1.0, None, ALU.add))
            link(v.reciprocal(wk[:, 0, :], wtmp[:, 2, :]))
            link(v.tensor_tensor(wk[:, 1, :], wk[:, 0, :], wtmp[:, 1, :], ALU.mult))

            v.wait_ge(prefixed, 2)
            ps, tot = (YF[1][:, n * 256:n * 256 + 256] for n in (0, 1))
            link(v.tensor_tensor_scan(upto[:].rearrange("p e j -> p (e j)"), restart[:].rearrange("p e j -> p (e j)"),
                                      tot, 0.0, ALU.mult, ALU.add))
            link(v.tensor_tensor(full[:], upto[:, :, BLOCKS - 1:BLOCKS].broadcast_to([P, E, 16]),
                                 step_iota[:, None, :].broadcast_to([P, E, 16]), ALU.is_gt))
            link(v.tensor_reduce(units[:], full[:], AX.X, ALU.add))
            link(v.tensor_tensor_scan(units_to[:], ones[:, 0:E], units[:], 0.0, ALU.mult, ALU.add))
            link(v.tensor_tensor(first[:], units_to[:], units[:], ALU.subtract))
            v.tensor_tensor(posn[:], upto[:], tot.rearrange("p (e j) -> p e j", e=E), ALU.subtract)
            link(v.tensor_scalar(first[:], first[:], float(P), None, ALU.mult))
            link(v.tensor_tensor(posn[:], posn[:], first[:, :, None].broadcast_to([P, E, BLOCKS]), ALU.add))
            link(v.tensor_tensor(posn[:], posn[:], ps.rearrange("p (e j) -> p e j", e=E), ALU.add))
            link(v.tensor_tensor(posn[:], posn[:], chosen[:].rearrange("p k i e -> p e (k i)"), ALU.mult))
            link(v.tensor_reduce(pos[:], posn[:].rearrange("p e j -> p j e"), AX.X, ALU.add))
            link(v.tensor_copy(pos_i[:], pos[:]))
            v.tensor_scalar(pu_i[:], pos_i[:], 7, None, ALU.logical_shift_right)
            link(v.tensor_scalar(pr_i[:], pos_i[:], P - 1, None, ALU.bitwise_and))
            v.tensor_copy(pu[:], pu_i[:])
            link(v.tensor_copy(pr[:], pr_i[:]))
            per_unit = [P, BLOCKS, UNITS]
            v.tensor_tensor(in_unit[:], pu[:, :, None].broadcast_to(per_unit),
                            unit_iota[:, None, 0:UNITS].broadcast_to(per_unit), ALU.is_equal).then_inc(rows_made, 1)
            v.wait_ge(rows_made, 1)
            v.tensor_scalar(from_who[:, :, 0, :], in_unit[:], part_iota[:], None, ALU.mult)
            for q in range(4):
                part = slice(q * BLOCKS // 4, (q + 1) * BLOCKS // 4)
                per_row = [P, BLOCKS // 4, P]
                v.tensor_tensor(in_row[:, part, :], pr[:, part, None].broadcast_to(per_row),
                                row_iota[:, None, :].broadcast_to(per_row), ALU.is_equal).then_inc(posed, 1)
            every = [1, UNITS + 2, E]
            link(v.tensor_tensor(past[:], units_to[0:1, None, :].broadcast_to(every),
                                 unit_iota[0:1, :, None].broadcast_to(every), ALU.is_le))
            link(v.tensor_reduce(who[:], past[:], AX.X, ALU.add))
            link(v.tensor_scalar(who[:], who[:], float(E - 1), float(WCOLS), ALU.min, ALU.mult))
            v.tensor_copy(who_i[:, 0:UNITS + 2], who[:]).then_inc(who_made, 1)

            def add_shared(g):
                v.wait_ge(sh2, g + 1)
                v.wait_ge(acc_made, g + 1)
                v.tensor_tensor(acc[:, tiles(g), :], acc[:, tiles(g), :],
                                YF[0][:].rearrange("p (i c) -> p i c", c=C), ALU.add).then_inc(sh_added, 1)

            add_shared(0)
            v.wait_ge(inv_done, 1)
            link(v.tensor_copy(inv[:].rearrange("p n u -> p (n u)"), LB[:, P:P + 2 * UNITS]))
            v.scalar_tensor_tensor(spare[:], inv[:, 1, :], 0.0, spare_iota[:], ALU.is_equal, ALU.mult)
            link(v.scalar_tensor_tensor(dest[:], inv[:, 1, :], float(P), inv[:, 0, :], ALU.mult, ALU.add))
            link(v.scalar_tensor_tensor(dest[:], dest[:], -float(P), spare[:], ALU.add, ALU.add))
            v.tensor_copy(dest_u[:], dest[:]).then_inc(idx_made, 1)
            v.wait_ge(idx_made, 1)
            v.tensor_scalar(tok_u[:], dest_u[:], TOKENS - 1, None, ALU.bitwise_and).then_inc(idx_made, 1)

            def set_weights(off, b):
                v.tensor_copy(wring[:, b, :], exw_s[:, bass.ds(off, WCOLS)]).then_inc(w_set, 1)

            def take_x(u, b):
                v.wait_ge(turned_x, u + 1)
                v.tensor_copy(xgt[:, b, :], TB[:, 0:P]).then_inc(xgt_made, 1)

            def take_y(u, b, landed):
                v.wait_ge(s2_done, u + 1)
                if landed is not None:
                    v.wait_ge(scattered[b], landed)
                v.tensor_tensor(ys[:, b, :], YB[:, 0:C], wring[:, b, OB2:], ALU.add).then_inc(ys_made, 1)

            regs = [v.alloc_register(f"offset{n}") for n in range(ROUND)]

            def offsets(u, n):
                v.load(regs[0:n], who_i[0:1, bass.ds(u, n)])
                return [v.snap(r, min_val=0, max_val=(E - 1) * WCOLS) for r in regs[0:n]]

            def unit(u, n, landed, off):
                if n + 1 < UNITS:
                    take_x(u + 1, (n + 1) % RING)
                if n:
                    take_y(u - 1, (n - 1) % RING, landed)
                if off is not None:
                    if n:
                        v.wait_ge(ys_made, u)
                    set_weights(off, (n + 2) % RING)

            def landed(n):
                return 16 * ((n - 1) // RING) if n > RING else None

            v.wait_ge(ld_ex, 32)
            v.wait_ge(who_made, 1)
            for b, off in enumerate(offsets(0, 2)):
                set_weights(off, b)
            add_shared(1)
            add_shared(2)
            take_x(0, 0)
            add_shared(3)
            offs = offsets(2, ROUND)
            for u in range(ROUND):
                unit(u, u, landed(u), offs[u])
            with v.Fori(1, ROUNDS) as r:
                offs = offsets(r * ROUND + 2, ROUND)
                for n in range(ROUND):
                    per_round = 16 * ROUND // RING
                    unit(r * ROUND + n, ROUND + n, r * per_round + (landed(ROUND + n) - per_round), offs[n])
            offs = offsets(ROUND * ROUNDS + 2, UNITS - ROUND * ROUNDS - 2) + [None, None]
            for u in range(ROUND * ROUNDS, UNITS):
                unit(u, u, landed(u), offs[u - ROUND * ROUNDS])
            take_y(UNITS - 1, (UNITS - 1) % RING, landed(UNITS))

            for g in range(GROUPS):
                v.wait_ge(ld_y[g], 32)
                for k in range(K):
                    for i in range(TG * g, TG * g + TG):
                        ins = v.scalar_tensor_tensor(acc[:, i, :], yk[k][:, i, :], wk[:, k, i:i + 1], acc[:, i, :],
                                                     ALU.mult, ALU.add)
                        if k == K - 1:
                            ins.then_inc(summed, 1)
                    if k == 0:
                        link(v.tensor_copy(pause[:], wk[:, 0, 0:1]))

        @block.tensor
        def _(pe):
            def transposes(dst, src, g, ready, signal):
                pe.wait_ge(ready, TG * (g + 1))
                for i in range(TG):
                    ins = pe.transpose(dst[:, i * P:i * P + P], src[:, TG * g + i, :], ident[:])
                ins.then_inc(signal, 1)

            def inputs(g):
                pe.wait_ge(xnt_made, g + 1)
                for n in range(2):
                    if g:
                        pe.wait_ge(turned, 2 * (g - 1) + n + 1)
                    pe.matmul(HB[n][:], bt_s[:, n, :], xnt[:, toks(g)], start=True, stop=True).then_inc(bu_done, 1)

            def outputs(g):
                if g:
                    pe.wait_ge(x1_made, g)
                pe.wait_ge(u1_made, g + 1)
                pe.wait_ge(u2_made, g + 1)
                for i in range(TG):
                    tok = slice(i * P, i * P + P)
                    o = YF[0][:, i * C:i * C + C]
                    pe.matmul(o, xnt[:, GT * g + i * P:GT * g + i * P + P], dt_s[:], start=True, stop=False)
                    pe.matmul(o, t1[:, g, tok], cw[:, 0, :], start=False, stop=False)
                    ins = pe.matmul(o, t2[:, g, tok], cw[:, 1, :], start=False, stop=True)
                ins.then_inc(y_done, 1)

            def router(g):
                pe.wait_ge(xn2t_made, g + 1)
                if g:
                    pe.wait_ge(h1_made, g)
                else:
                    pe.wait_ge(ld_r, 64)
                pe.matmul(HB[2][0:R, :], wr1_s[:], xn2t[:, toks(g)], start=True, stop=True).then_inc(h1_done, 1)

            def logits(g):
                pe.wait_ge(h1_made, g + 1)
                for i in range(TG * g, TG * g + TG):
                    ins = pe.matmul(LB[:, i * E:i * E + E], h1[:, i * P:i * P + P], wr2_s[:], start=True, stop=True)
                ins.then_inc(lg_done, 1)

            pe.wait_ge(cst, 8)
            for k in range(GROUPS + 4):
                if 2 <= k < GROUPS + 2:
                    if k == 2:
                        pe.wait_ge(ld_c, 32)
                        pe.wait_ge(tabled, 3)
                    outputs(k - 2)
                if k >= 4:
                    logits(k - 4)
                if 2 <= k < GROUPS + 2 and k % SEQ_GROUPS == 0:
                    pe.matmul(LB[:, GT - 1:GT], carry[:], zs[:, k - 2, GT - 1:GT], start=True, stop=True).then_inc(carried, 1)
                if 1 <= k <= GROUPS:
                    if k == 1:
                        pe.wait_ge(ld_b, 16)
                    inputs(k - 1)
                if 3 <= k < GROUPS + 3:
                    router(k - 3)
                if k < GROUPS:
                    if k:
                        pe.wait_ge(xnt_made, k)
                    transposes(TB, xn, k, xn1_made, t1_done)
                if 2 <= k < GROUPS + 2:
                    if k > 2:
                        pe.wait_ge(xn2t_made, k - 2)
                    transposes(YB, xn, k - 2, xn2_made, t2_done)

            def shared_1(g):
                for c in range(IC):
                    n = g * IC + c
                    if n == 0:
                        pe.wait_ge(ld_sh, 32)
                        pe.wait_ge(turned, 2 * GROUPS)
                    if n >= 3:
                        pe.wait_ge(sh_act, n - 2)
                    pe.matmul(HB[n % 3][:], shw_s[:, c * P:c * P + P], xn2t[:, toks(g)],
                              start=True, stop=True).then_inc(sh1, 1)

            def shared_2(g):
                pe.wait_ge(sh_act, IC * (g + 1))
                if g:
                    pe.wait_ge(sh_added, g)
                else:
                    pe.wait_ge(x1_made, GROUPS)
                for i in range(TG):
                    for c in range(IC):
                        ins = pe.matmul(YF[0][:, i * C:i * C + C], hs[:, g % 2, c, i * P:i * P + P],
                                        shw_s[:, OW2 + c * C:OW2 + c * C + C], start=(c == 0), stop=(c == IC - 1))
                ins.then_inc(sh2, 1)

            shared_1(0)
            pe.wait_ge(cst, CONSTS)
            pe.wait_ge(routed, 1)
            rows = chosen[:].rearrange("p k i e -> p e (k i)")
            for n, lhs in enumerate((before, ones)):
                pe.matmul(YF[1][:, n * 256:n * 256 + 256], lhs[:], rows, start=True, stop=True).then_inc(prefixed, 1)
            shared_1(1)
            shared_2(0)
            pe.wait_ge(blocks_made, 1)
            pe.wait_ge(posed, 4)
            for j in range(BLOCKS):
                ins = pe.matmul(LB[:, P:P + 2 * UNITS], in_row[:, j, :], from_who[:, j, :, :].rearrange("p n u -> p (n u)"),
                                start=(j == 0), stop=(j == BLOCKS - 1))
            ins.then_inc(inv_done, 1)
            shared_1(2)
            shared_2(1)
            shared_1(3)
            shared_2(2)

            def turn_x(u, n, landed):
                pe.wait_ge(gathered[n % AHEAD], landed)
                if n:
                    pe.wait_ge(xgt_made, u)
                else:
                    pe.wait_ge(xnt_made, GROUPS)
                pe.transpose(TB[:, 0:P], xg[:, n % AHEAD, :], ident[:]).then_inc(turned_x, 1)

            def up(u, n):
                b = n % RING
                if n == 0:
                    pe.wait_ge(sh_act, IC * GROUPS)
                    pe.wait_ge(sh_added, GROUPS)
                pe.wait_ge(w_set, u + 1)
                pe.wait_ge(xgt_made, u + 1)
                for c in range(IC):
                    ins = pe.matmul(HU[b][c // 2][:, c % 2 * P:c % 2 * P + P], wring[:, b, c * P:c * P + P],
                                    xgt[:, b, :], start=True, stop=True)
                    if c % 2:
                        ins.then_inc(s1_done, 1)

            def down(u, n):
                b = n % RING
                if n:
                    pe.wait_ge(ys_made, u)
                else:
                    pe.wait_ge(xn2t_made, GROUPS)
                for c in range(IC):
                    pe.wait_ge(h_made, u * IC + c + 1)
                    ins = pe.matmul(YB[:, 0:C], he[:, b, c, :], wring[:, b, OW2 + c * C:OW2 + c * C + C],
                                    start=(c == 0), stop=(c == IC - 1))
                ins.then_inc(s2_done, 1)

            def unit(u, n, landed):
                if n + 1 < UNITS:
                    turn_x(u + 1, n + 1, landed)
                up(u, n)
                if n:
                    down(u - 1, n - 1)

            def landed(n):
                return 16 * (n // AHEAD + 1)

            turn_x(0, 0, landed(0))
            shared_2(3)
            for u in range(ROUND):
                unit(u, u, landed(u + 1))
            with pe.Fori(1, ROUNDS) as r:
                for n in range(ROUND):
                    per_round = 16 * ROUND // AHEAD
                    unit(r * ROUND + n, ROUND + n, r * per_round + (landed(ROUND + n + 1) - per_round))
            for u in range(ROUND * ROUNDS, UNITS):
                unit(u, u, landed(u + 1))
            down(UNITS - 1, UNITS - 1)


def kernel(**inputs):
    import numpy as np
    import concourse.bacc as bacc
    from concourse.bass_utils import run_bass_kernel_spmd

    a = {name.replace("L0_", ""): np.asarray(value) for name, value in inputs.items()}

    def down(w):
        return w.reshape(IC, P, C).transpose(1, 0, 2).reshape(P, IC * C)

    arrays = {
        "x": a["attn_x"],
        "prm": np.tile(np.stack([a["attn_nu_log"], a["attn_theta_log"], a["attn_gamma_log"]], 1), (2, 1)),
        "bt": np.stack([np.concatenate([a["attn_B_re"], a["attn_B_im"]]).T,
                        np.concatenate([a["attn_B_im"], a["attn_B_re"]]).T], 1),
        "ct": np.stack([np.concatenate([a["attn_C_re"], a["attn_C_im"]], 1).T,
                        np.concatenate([a["attn_C_im"], a["attn_C_re"]], 1).T], 1),
        "dt": a["attn_D"].T,
        "wr1": a["ffn_Wr1"],
        "br1": a["ffn_br1"][:, None],
        "wr2": a["ffn_Wr2"],
        "br2": a["ffn_br2"][None],
        "shw": np.concatenate([a["ffn_Ws1"], down(a["ffn_Ws2"]), a["ffn_bs1"].reshape(IC, P).T], 1),
        "bs2": a["ffn_bs2"][None],
        "exw": np.stack([np.concatenate([a["ffn_We1"][e], down(a["ffn_We2"][e]), a["ffn_be1"][e].reshape(IC, P).T], 1)
                         for e in range(E)], 1),
        "be2": a["ffn_be2"][None],
    }
    nc = bacc.Bacc("TRN2", target_bir_lowering=False, num_devices=1)
    feeds, aps = {}, []
    for name, value in arrays.items():
        feeds[f"in_{name}"] = np.ascontiguousarray(value)
        aps.append(nc.dram_tensor(f"in_{name}", value.shape, mybir.dt.from_np(value.dtype), kind="ExternalInput").ap())
    shape = a["attn_x"].shape
    aps.append(nc.dram_tensor("out_x", shape, F32, kind="ExternalOutput").ap())
    seq_moe_kernel(nc, *aps)
    r = run_bass_kernel_spmd(nc, [feeds], core_ids=[0])
    return r.results[0]["out_x"]
```

```python
from contextlib import ExitStack

import concourse.bass as bass
from concourse import mybir

F32 = mybir.dt.float32
F32R = mybir.dt.float32r
BF16 = mybir.dt.bfloat16
I32 = mybir.dt.int32
U32 = mybir.dt.uint32
ALU = mybir.AluOpType
ACT = mybir.ActivationFunctionType
AX = mybir.AxisListType

P = 128
TILES = 16
GROUPS = 4
TG = TILES // GROUPS
GT = TG * P
SEQ_GROUPS = 2
NS = 64
C = 128
I = 512
IC = I // P
E = 8
K = 2
R = 32
TOKENS = TILES * P
BLOCKS = K * TILES
UNITS = K * TOKENS // P + E - 1
RING = 3
AHEAD = 12
LAG = (8, 6, 9)
ROUND = 12
ROUNDS = UNITS // ROUND
FINE = 32
COARSE = GT // FINE
OW2, OB1, OB2, WCOLS = I, 2 * I, 2 * I + IC, 2 * I + IC + C
EPS = 1e-5
WARM_UP = 5
TO_INT = 12582912.0
TWO_PI_HI, TWO_PI_LO = 6.28125, 0.0019353071795864769
PI_DOWN = 3.1415925
TOP_12 = 0xFFFFF000
assert LAG[0] < AHEAD and ROUND % RING == 0 and ROUND % AHEAD == 0 and UNITS % RING == 0


def seq_moe_kernel(nc, x, prm, bt, ct, dt, wr1, br1, wr2, shw, bs2, exw, be2, out):
    xn_dram = nc.dram_tensor("xn_rows", [TOKENS, C], F32, kind="Internal").ap()
    y_dram = nc.dram_tensor("y_rows", [K * TOKENS + UNITS * P, C], F32, kind="Internal").ap()

    with ExitStack() as ctx:
        def sb(name, shape, dtype=F32):
            return ctx.enter_context(nc.sbuf_tensor(name, shape, dtype))

        def sem(name):
            return ctx.enter_context(nc.semaphore(name))

        ident = sb("ident", [P, P])
        before = sb("before", [P, P], BF16)
        ones = sb("ones", [P, P], BF16)
        swap = sb("swap", [P, P])
        row_iota = sb("row_iota", [P, P], BF16)
        unit_iota = sb("unit_iota", [P, UNITS + 2])
        block_iota = sb("block_iota", [P, BLOCKS])
        part_iota = sb("part_iota", [P, 1])
        step_iota = sb("step_iota", [P, TOKENS // P])
        spare_iota = sb("spare_iota", [P, UNITS])
        rank_iota = sb("rank_iota", [P, E])
        restart = sb("restart", [P, E, BLOCKS])
        euler = sb("euler", [P, 1])
        inv_euler = sb("inv_euler", [P, 1])
        neg_half = sb("neg_half", [P, TG])
        sign = sb("sign", [P, 1])
        zeros = sb("zeros", [P, GT], BF16)
        half_pi = sb("half_pi", [P, 1])
        prm_s = sb("prm_s", [P, 3])
        bt_s = sb("bt_s", [P, 2, P])
        ct_s = sb("ct_s", [P, 2, C])
        cw = sb("cw", [P, 2, C])
        dt_s = sb("dt_s", [P, C])
        wr1_s = sb("wr1_s", [P, R])
        br1_s = sb("br1_s", [R, 1])
        wr2_s = sb("wr2_s", [R + 1, E])
        shw_s = sb("shw_s", [P, OB2])
        bs2_s = sb("bs2_s", [P, C])
        w1_parts = [sb(f"w1_part{n}", [P, I], F32R) for n in range(2)]
        exw_s = sb("exw_s", [P, E * WCOLS])
        pw = sb("pw", [P, 5])
        ang = sb("ang", [P, 8])
        steps = sb("steps", [P, FINE + COARSE + 1])
        angs = sb("angs", [P, 4, FINE + COARSE + 1])
        turns = sb("turns", [P, 2, FINE + COARSE + 1])
        pause = sb("pause", [P, 1])
        quiet = sb("quiet", [P, 2])
        cos = sb("cos", [P, GT])
        sin = sb("sin", [P, GT])
        cos_t = sb("cos_t", [P, GT])
        sin_t = sb("sin_t", [P, GT])
        carry = sb("carry", [P, P])
        fine, coarse = turns[:, :, 0:FINE], turns[:, :, FINE:]
        xs = sb("xs", [P, TILES, C])
        xn = sb("xn", [P, TILES, C])
        xnt = sb("xnt", [P, TOKENS])
        x1 = sb("x1", [P, TILES, C])
        acc = xs
        xn2t = sb("xn2t", [P, TOKENS])
        bn = sb("bn", [P, 2, TILES, 6])
        mv = sb("mv", [P, 2, TILES, 2])
        veps = sb("veps", [P, 2, TILES])
        rstd = sb("rstd", [P, 2, TILES])
        xsum, nmean, xsq, shift = (sb(n, [P, TILES]) for n in ("xsum", "nmean", "xsq", "shift"))
        t1 = sb("t1", [P, GROUPS, GT])
        t2 = sb("t2", [P, GROUPS, GT])
        zs = sb("zs", [P, GROUPS, GT])
        h1 = sb("h1", [R + 1, TOKENS])
        x_parts = [sb(f"x_part{n}", [P, GROUPS - 1, GT], F32R) for n in range(2)]
        lg = sb("lg", [P, TILES, E])
        lmax = sb("lmax", [P, TILES])
        gates = sb("gates", [P, TILES, E])
        rest = sb("rest", [P, TILES, E])
        pick = sb("pick", [P, TILES, E])
        gsum = sb("gsum", [P, TILES])
        ginv = sb("ginv", [P, TILES])
        top = sb("top", [P, K, TILES])
        key = sb("key", [P, TILES])
        wk = sb("wk", [P, K, TILES])
        wtmp = sb("wtmp", [P, 3, TILES])
        chosen = sb("chosen", [P, K, TILES, E], BF16)
        upto = sb("upto", [P, E, BLOCKS])
        posn = sb("posn", [P, E, BLOCKS])
        full = sb("full", [P, E, 16])
        unit_count = sb("unit_count", [P, E + 1])
        units_to = sb("units_to", [P, E + 1])
        pos = sb("pos", [P, BLOCKS])
        pos_i = sb("pos_i", [P, BLOCKS], I32)
        pu_i = sb("pu_i", [P, BLOCKS], I32)
        pr_i = sb("pr_i", [P, BLOCKS], I32)
        pu = sb("pu", [P, BLOCKS])
        pr = sb("pr", [P, BLOCKS])
        in_row = zs[:].rearrange("p g t -> p (g t)").bitcast(BF16).rearrange("p (j r) -> p j r", r=P)
        spot = xnt[:].bitcast(BF16)
        in_unit = spot[:, 0:BLOCKS * UNITS].rearrange("p (j u) -> p j u", u=UNITS)
        from_who = spot[:, BLOCKS * UNITS:3 * BLOCKS * UNITS].rearrange("p (j n u) -> p j n u", n=2, u=UNITS)
        inv = sb("inv", [P, UNITS])
        spare = sb("spare", [P, UNITS])
        dest = sb("dest", [P, UNITS])
        dest_u = sb("dest_u", [P, UNITS], U32)
        tok_i = sb("tok_i", [P, UNITS], U32)
        tok_u = sb("tok_u", [P, UNITS], U32)
        past = sb("past", [1, UNITS + 2, E])
        who = sb("who", [1, UNITS + 2])
        who_i = sb("who_i", [1, UNITS + 2], I32)
        hs = sb("hs", [P, 2, IC, GT])
        wring = sb("wring", [P, RING, WCOLS])
        xg = sb("xg", [P, AHEAD, C])
        xgt = sb("xgt", [P, RING, P])
        he = sb("he", [P, RING, IC, P])
        ys = sb("ys", [P, RING, C])
        yk = [t[:].rearrange("p g (i c) -> p (g i) c", c=C) for t in (t1, t2)]

        bank = [ctx.enter_context(nc.psum_tensor(f"bank{i}", [P, GT], F32)) for i in range(8)]
        HB = bank[0:3]
        HU = [(bank[0], bank[7]), (bank[1], bank[6]), (bank[2], bank[5])]
        TB, YB = bank[3], bank[4]
        YF = (bank[5], bank[7])
        RH = (bank[6], bank[3])
        RB = bank[6]
        LB = bank[7]
        SB = (bank[5], YB, bank[6], bank[5])

        ld_x = [sem(f"ld_x{g}") for g in range(GROUPS)]
        ld_prm, ld_b, ld_c, ld_r, ld_sh, ld_ex = (sem(n) for n in ("ld_prm", "ld_b", "ld_c", "ld_r", "ld_sh", "ld_ex"))
        zeroed = sem("zeroed")
        cst, powed, sined, angled, tabled, sin_made = (sem(n) for n in ("cst", "powed", "sined", "angled", "tabled", "sin_made"))
        act_steps, pool_steps, squared = (sem(n) for n in ("act_steps", "pool_steps", "squared"))
        stats1, rstd1, xn1_made, t1_done, xnt_made = (sem(n) for n in ("stats1", "rstd1", "xn1_made", "t1_done", "xnt_made"))
        bu_done, turned, scanned, u1_made, u2_made, carried = (sem(n) for n in ("bu_done", "turned", "scanned", "u1_made", "u2_made", "carried"))
        y_done, x1_made, stats2, rstd2, xn2_made, t2_done, xn2t_made = (sem(n) for n in ("y_done", "x1_made", "stats2", "rstd2", "xn2_made", "t2_done", "xn2t_made"))
        acc_made, h1_done, h1_made, lg_done, xn_stored = (sem(n) for n in ("acc_made", "h1_done", "h1_made", "lg_done", "xn_stored"))
        dve, lmaxed, exped, wdiff, routed, prefixed, posed, who_made, rows_made, inv_done, idx_made = (
            sem(n) for n in ("dve", "lmaxed", "exped", "wdiff", "routed", "prefixed", "posed", "who_made", "rows_made", "inv_done", "idx_made"))
        blocks_made, parts_made = sem("blocks_made"), sem("parts_made")
        high_made, low_made = sem("high_made"), sem("low_made")
        sh1, sh_act, sh2, sh_added = (sem(n) for n in ("sh1", "sh_act", "sh2", "sh_added"))
        gathered = [sem(f"gathered{b}") for b in range(AHEAD)]
        scattered = [sem(f"scattered{b}") for b in range(RING)]
        turned_x, xgt_made, s1_done, h_made, s2_done, ys_made, w_set = (
            sem(n) for n in ("turned_x", "xgt_made", "s1_done", "h_made", "s2_done", "ys_made", "w_set"))
        ld_y = [[sem(f"ld_y{k}_{g}") for g in range(GROUPS)] for k in range(K)]
        wk_made, weighted, added = sem("wk_made"), sem("weighted"), sem("added")
        posed_by_pool = sem("posed_by_pool")
        summed, stored = sem("summed"), sem("stored")

        CONSTS = 22
        HALVES = (slice(0, BLOCKS // 2), slice(BLOCKS // 2, BLOCKS))
        DVE_ROWS = BLOCKS - 5
        y_view = y_dram[0:K * TOKENS, :].rearrange("(k i p) c -> p k i c", k=K, p=P)
        x_view = x.rearrange("b (i p) c -> p (b i) c", p=P)
        out_view = out.rearrange("b (i p) c -> p (b i) c", p=P)
        xn_view = xn_dram.rearrange("(i p) c -> p i c", p=P)

        def tiles(g):
            return slice(TG * g, TG * g + TG)

        def toks(g):
            return slice(GT * g, GT * g + GT)

        block = ctx.enter_context(nc.Block())

        @block.sync
        def _(sp):
            sp.dma_start(prm_s[:], prm).then_inc(ld_prm, 16)
            for g in range(GROUPS):
                sp.dma_start(xs[:, tiles(g), :], x_view[:, tiles(g), :]).then_inc(ld_x[g], 16)
                if g == 0:
                    sp.dma_start(bt_s[:], bt).then_inc(ld_b, 16)
            sp.dma_start(ct_s[:], ct).then_inc(ld_c, 16)
            sp.dma_start(dt_s[:], dt).then_inc(ld_c, 16)
            sp.dma_start(wr1_s[:], wr1).then_inc(ld_r, 16)
            sp.dma_start(br1_s[:], br1).then_inc(ld_r, 16)
            sp.dma_start(wr2_s[:], wr2).then_inc(ld_r, 16)
            sp.dma_start(bs2_s[:], bs2.broadcast_to([P, C])).then_inc(ld_sh, 16)
            sp.dma_start(shw_s[:], shw).then_inc(ld_sh, 16)
            ex = exw_s[:].rearrange("p (e w) -> p e w", e=E)
            sp.dma_start(ex[:, :, OB2:], be2.broadcast_to([P, E, C])).then_inc(ld_ex, 16)
            sp.dma_start(ex[:, :, 0:OB2], exw).then_inc(ld_ex, 16)
            for g in range(GROUPS):
                sp.wait_ge(xn2_made, g + 1)
                sp.dma_start(xn_view[:, tiles(g), :], xn[:, tiles(g), :]).then_inc(xn_stored, 16)
            for b in range(RING):
                sp.wait_ge(scattered[b], 16 * (UNITS // RING))
            for g in range(GROUPS):
                for k in range(K):
                    sp.dma_start(yk[k][:, tiles(g), :], y_view[:, k, tiles(g), :]).then_inc(ld_y[k][g], 16)
            for g in range(GROUPS):
                if g < GROUPS - 1:
                    sp.wait_ge(summed, g + 1)
                else:
                    sp.wait_ge(added, GROUPS)
                sp.dma_start(out_view[:, tiles(g), :], acc[:, tiles(g), :]).then_inc(stored, 16)
            sp.wait_ge(stored, 16 * GROUPS)
            sp.wait_ge(xn_stored, 16 * GROUPS)

        @block.gpsimd
        def _(pool):
            pool.memset(euler[:], 2.718281828459045).then_inc(cst, 1)
            pool.memset(inv_euler[:], 0.36787944117144233).then_inc(cst, 1)
            pool.memset(neg_half[:], -0.5).then_inc(cst, 1)
            pool.memset(half_pi[:], 1.5707963267948966).then_inc(cst, 1)
            pool.iota(steps[:, 0:FINE], [[1, FINE]], base=1, channel_multiplier=0,
                      allow_small_or_imprecise_dtypes=True).then_inc(cst, 1)
            pool.iota(steps[:, FINE:], [[FINE, COARSE + 1]], base=0, channel_multiplier=0,
                      allow_small_or_imprecise_dtypes=True).then_inc(cst, 1)
            pool.wait_ge(ld_prm, 16)
            pool.wait_ge(cst, 4)
            pool.tensor_tensor(pw[:, 0:1], euler[:], prm_s[:, 1:2], ALU.pow).then_inc(powed, 1)
            pool.tensor_tensor(pw[:, 1:2], euler[:], prm_s[:, 0:1], ALU.pow).then_inc(powed, 1)
            pool.tensor_tensor(pw[:, 3:4], euler[:], prm_s[:, 2:3], ALU.pow).then_inc(powed, 1)
            pool.wait_ge(powed, 3)
            pool.tensor_tensor(pw[:, 2:3], inv_euler[:], pw[:, 1:2], ALU.pow).then_inc(powed, 1)
            pool.memset(ident[:], 0.0).then_inc(cst, 1)
            pool.wait_ge(cst, 7)
            pool.affine_select(out=ident[:], in_=ident[:], compare_op=ALU.not_equal, fill=1.0, base=0,
                               pattern=[[-1, P]], channel_multiplier=1).then_inc(cst, 1)

            def rstd_of(n, g, signal, ready):
                pool.wait_ge(ready, g + 1)
                pool.tensor_tensor(rstd[:, n, tiles(g)], veps[:, n, tiles(g)], neg_half[:], ALU.pow).then_inc(signal, 1)

            def rstd_from_sums(g):
                pool.wait_ge(squared, g)
                pool.tensor_scalar(veps[:, 0, tiles(g)], xsq[:, tiles(g)], 1.0 / C, EPS, ALU.mult, ALU.add).then_inc(pool_steps, 1)
                pool.wait_ge(pool_steps, 2 * g - 1)
                pool.tensor_tensor(rstd[:, 0, tiles(g)], veps[:, 0, tiles(g)], neg_half[:], ALU.pow).then_inc(pool_steps, 1)
                pool.wait_ge(pool_steps, 2 * g)
                pool.tensor_tensor(shift[:, tiles(g)], nmean[:, tiles(g)], rstd[:, 0, tiles(g)], ALU.mult).then_inc(rstd1, 1)

            def turn_back(g):
                pool.wait_ge(scanned, g + 1)
                pool.tensor_tensor(t2[:, g, :], sin[:], zs[:, g, :], ALU.mult).then_inc(u2_made, 1)

            def start_acc(g):
                if g == 0:
                    pool.wait_ge(ld_sh, 32)
                pool.wait_ge(x1_made, g + 1)
                pool.tensor_tensor(acc[:, tiles(g), :], x1[:, tiles(g), :],
                                   bs2_s[:, None, :].broadcast_to([P, TG, C]), ALU.add).then_inc(acc_made, 1)

            rstd_of(0, 0, rstd1, stats1)
            rstd_from_sums(1)
            pool.wait_ge(sined, 2)
            shape = [P, COARSE, FINE]
            cc, cs = (coarse[:, n, 0:COARSE][:, :, None].broadcast_to(shape) for n in (0, 1))
            fc, fs = (fine[:, n, None, :].broadcast_to(shape) for n in (0, 1))
            grid = [t[:].rearrange("p (m j) -> p m j", j=FINE) for t in (sin, sin_t)]
            pool.tensor_tensor(grid[0], cc, fs, ALU.mult).then_inc(sin_made, 1)
            pool.tensor_tensor(grid[1], cs, fc, ALU.mult).then_inc(sin_made, 1)
            pool.memset(swap[:], 0.0).then_inc(cst, 1)
            pool.wait_ge(cst, 9)
            pool.affine_select(out=swap[:], in_=swap[:], compare_op=ALU.not_equal, fill=1.0, base=NS,
                               pattern=[[-1, P]], channel_multiplier=1).then_inc(cst, 1)
            pool.wait_ge(cst, 10)
            pool.affine_select(out=swap[:], in_=swap[:], compare_op=ALU.not_equal, fill=-1.0, base=-NS,
                               pattern=[[-1, P]], channel_multiplier=1).then_inc(cst, 1)
            turn_back(0)
            rstd_from_sums(2)
            pool.memset(ones[:], 1.0).then_inc(cst, 1)
            pool.wait_ge(cst, 12)
            pool.affine_select(out=before[:], in_=ones[:], compare_op=ALU.is_gt, fill=0.0, base=0,
                               pattern=[[1, P]], channel_multiplier=-1).then_inc(cst, 1)
            for t, n, step, base, cm in (
                (row_iota, P, 1, 0, 0), (unit_iota, UNITS + 2, 1, 0, 0), (block_iota, BLOCKS, 1, 1, 0),
                (part_iota, 1, 1, 0, 1), (step_iota, TOKENS // P, P, 0, 0),
                (spare_iota, UNITS, P, K * TOKENS + P, 1), (rank_iota, E, -1, E, 0),
            ):
                pool.iota(t[:], [[step, n]], base=base, channel_multiplier=cm,
                          allow_small_or_imprecise_dtypes=True).then_inc(cst, 1)
            pool.memset(restart[:], 1.0).then_inc(cst, 1)
            pool.wait_ge(cst, 21)
            pool.memset(restart[:, :, 0:1], 0.0).then_inc(cst, 1)
            for g in range(1, GROUPS + 1):
                if g < GROUPS:
                    turn_back(g)
                if g == 1:
                    rstd_from_sums(3)
                rstd_of(1, g - 1, rstd2, stats2)
            pool.wait_ge(ld_sh, 32)
            pool.wait_ge(high_made, 1)
            pool.tensor_tensor(w1_parts[1][:], shw_s[:, 0:I], w1_parts[0][:].bitcast(F32), ALU.subtract).then_inc(low_made, 1)
            for g in range(1, GROUPS):
                pool.wait_ge(high_made, g + 1)
                pool.tensor_tensor(x_parts[1][:, g - 1, :], xn2t[:, toks(g)], x_parts[0][:, g - 1, :].bitcast(F32),
                                   ALU.subtract).then_inc(low_made, 1)
            for g in range(GROUPS):
                start_acc(g)

            for half, blocks in enumerate(HALVES):
                pool.wait_ge(rows_made, half + 1)
                pool.tensor_tensor(from_who[:, blocks, 1, :], in_unit[:, blocks, :],
                                   block_iota[:, blocks, None].broadcast_to([P, BLOCKS // 2, UNITS]),
                                   ALU.mult).then_inc(blocks_made, 1)
            for j in range(DVE_ROWS, BLOCKS):
                pool.tensor_scalar(in_row[:, j, :], row_iota[:], pr[:, j:j + 1], None, ALU.is_equal).then_inc(posed_by_pool, 1)

            def gather(u):
                b = u % AHEAD
                if u == 0:
                    pool.wait_ge(idx_made, 1)
                    pool.wait_ge(xn_stored, 16 * GROUPS)
                if u >= AHEAD:
                    pool.wait_ge(turned_x, u - AHEAD + 1)
                pool.indirect_dma_start(xg[:, b, :], None, xn_dram,
                                        bass.IndirectOffsetOnAxis(tok_u[:, u:u + 1], 0)).then_inc(gathered[b], 16)

            def scatter(u):
                b = u % RING
                if u == 0:
                    pool.wait_ge(idx_made, 2)
                pool.wait_ge(ys_made, u + 1)
                pool.indirect_dma_start(y_dram, bass.IndirectOffsetOnAxis(dest_u[:, u:u + 1], 0),
                                        ys[:, b, :], None).then_inc(scattered[b], 16)

            ahead = 0
            for u in range(UNITS):
                while ahead < min(UNITS, u + 1 + max(LAG[1], LAG[0] - u // LAG[2])):
                    gather(ahead)
                    ahead += 1
                scatter(u)

            for g in range(GROUPS - 1):
                pool.wait_ge(weighted, g + 1)
                pool.wait_ge(added, g + 1)
                pool.tensor_tensor(acc[:, tiles(g), :], acc[:, tiles(g), :], yk[0][:, tiles(g), :], ALU.add).then_inc(summed, 1)

        @block.scalar
        def _(act):
            act.wait_ge(cst, 4)
            act.activation(quiet[:, 0:1], half_pi[:], ACT.Sin)
            def take_t1(g):
                act.wait_ge(t1_done, g + 1)
                act.copy(xnt[:, toks(g)], TB[:]).then_inc(xnt_made, 1)

            def take_t2(g):
                act.wait_ge(t2_done, g + 1)
                act.copy(xn2t[:, toks(g)], YB[:]).then_inc(xn2t_made, 1)

            def take_router(g):
                act.wait_ge(h1_done, g + 1)
                if g == 0:
                    act.wait_ge(ld_r, 48)
                act.activation(h1[0:R, toks(g)], RH[g % 2][0:R, :], ACT.Relu, bias=br1_s[:]).then_inc(h1_made, 1)

            def shared_silu(n):
                g, c = n // IC, n % IC
                act.wait_ge(sh1, n + 1)
                if g >= 2:
                    act.wait_ge(sh2, g - 1)
                act.activation(hs[:, g % 2, c, :], HB[n % 3][:], ACT.Silu,
                               bias=shw_s[:, OB1 + c:OB1 + c + 1]).then_inc(sh_act, 1)

            def sums(g):
                act.wait_ge(ld_x[g], 16)
                for i in range(TG * g, TG * g + TG):
                    ins = act.activation(xn[:, i, :], xs[:, i, :], ACT.Identity, accum_out=xsum[:, i:i + 1])
                ins.then_inc(act_steps, 1)
                act.wait_ge(act_steps, 2 * g - 1)
                act.activation(nmean[:, tiles(g)], xsum[:, tiles(g)], ACT.Copy, scale=-1.0 / C).then_inc(act_steps, 1)

            def squares(g):
                act.wait_ge(act_steps, 2 * g)
                for i in range(TG * g, TG * g + TG):
                    ins = act.activation(xn[:, i, :], xs[:, i, :], ACT.Square, bias=nmean[:, i:i + 1],
                                         accum_out=xsq[:, i:i + 1])
                ins.then_inc(squared, 1)

            def normalize(g):
                act.wait_ge(rstd1, g + 1)
                for i in range(TG * g, TG * g + TG):
                    ins = act.activation(xn[:, i, :], xs[:, i, :], ACT.Identity, bias=shift[:, i:i + 1],
                                         scale=rstd[:, 0, i:i + 1])
                ins.then_inc(xn1_made, 1)

            sums(1)
            squares(1)
            act.wait_ge(angled, 1)
            act.wait_ge(cst, 4)
            act.activation(turns[:, 1, :], angs[:, 2, :], ACT.Sin).then_inc(sined, 1)
            act.activation(turns[:, 0, :], angs[:, 3, :], ACT.Sin, bias=half_pi[:], scale=-1.0).then_inc(sined, 1)
            take_t1(0)
            normalize(1)
            sums(2)
            take_t1(1)
            squares(2)
            sums(3)
            normalize(2)
            take_t1(2)
            squares(3)
            normalize(3)
            take_t1(3)
            act.activation(quiet[:, 1:2], half_pi[:], ACT.Silu)
            take_t2(0)
            take_router(0)
            shared_silu(0)
            take_t2(1)
            shared_silu(1)
            take_router(1)
            take_t2(2)
            shared_silu(2)
            take_t2(3)
            take_router(2)
            take_router(3)

            act.wait_ge(lmaxed, 1)
            act.activation(gates[:], lg[:], ACT.Exp).then_inc(exped, 1)
            for n in range(3, 6):
                shared_silu(n)
            for n in range(6, IC * (GROUPS - 1)):
                if n == 9:
                    for half, blocks in enumerate(HALVES):
                        act.wait_ge(rows_made, half + 1)
                        act.activation(from_who[:, blocks, 0, :], in_unit[:, blocks, :], ACT.Copy,
                                       scale=part_iota[:]).then_inc(parts_made, 1)
                shared_silu(n)
            def unit(u, n):
                b = n % RING
                for c in range(IC):
                    if c % 2 == 0:
                        act.wait_ge(s1_done, u * 2 + c // 2 + 1)
                    act.activation(he[:, b, c, :], HU[b][c // 2][:, c % 2 * P:c % 2 * P + P], ACT.Silu,
                                   bias=wring[:, b, OB1 + c:OB1 + c + 1]).then_inc(h_made, 1)

            for u in range(ROUND):
                unit(u, u)
            act.wait_ge(wdiff, 1)
            act.activation(wtmp[:, 1, :], wtmp[:, 0, :], ACT.Tanh, scale=0.25).then_inc(exped, 1)
            with act.Fori(1, ROUNDS) as r:
                for n in range(ROUND):
                    unit(r * ROUND + n, n)
            for u in range(ROUND * ROUNDS, UNITS):
                unit(u, u)

            for n in range(IC * (GROUPS - 1), IC * GROUPS):
                shared_silu(n)

            act.wait_ge(wk_made, 1)
            for g in range(GROUPS):
                act.wait_ge(ld_y[0][g], 16)
                for i in range(TG * g, TG * g + TG):
                    ins = act.activation(yk[0][:, i, :], yk[0][:, i, :], ACT.Copy, scale=wk[:, 0, i:i + 1])
                ins.then_inc(weighted, 1)

        @block.vector
        def _(v):
            links = [0]

            def link(ins):
                links[0] += 1
                ins.then_inc(dve, 1)
                v.wait_ge(dve, links[0])

            def stats(n, g, src, signal):
                for i in range(TG * g, TG * g + TG):
                    ins = v.bn_stats(bn[:, n, i, :], src[:, i, :])
                link(ins)
                for i in range(TG * g, TG * g + TG):
                    ins = v.bn_aggr(mv[:, n, i, :], bn[:, n, i, :])
                link(ins)
                v.tensor_scalar(veps[:, n, tiles(g)], mv[:, n, tiles(g), 1], EPS, None, ALU.add).then_inc(signal, 1)

            def normalize(n, g, src, ready, signal):
                v.wait_ge(ready, g + 1)
                for i in range(TG * g, TG * g + TG):
                    ins = v.tensor_scalar(xn[:, i, :], src[:, i, :], mv[:, n, i, 0:1], rstd[:, n, i:i + 1],
                                          ALU.subtract, ALU.mult)
                ins.then_inc(signal, 1)

            v.memset(zeros[:], 0.0).then_inc(zeroed, 1)
            v.memset(h1[R:R + 1, :], 1.0).then_inc(zeroed, 1)
            v.memset(unit_count[:, 0:1], 0.0)
            v.memset(sign[0:NS, :], 1.0)
            v.memset(sign[NS:P, :], -1.0)
            v.wait_ge(ld_x[0], 16)
            stats(0, 0, xs, stats1)
            v.wait_ge(powed, 1)
            link(v.tensor_scalar(ang[:, 0:1].bitcast(U32), pw[:, 0:1].bitcast(U32), TOP_12, None, ALU.bitwise_and))
            v.tensor_scalar(ang[:, 2:3], pw[:, 0:1], 0.15915494309189535, None, ALU.mult)
            link(v.tensor_tensor(ang[:, 1:2], pw[:, 0:1], ang[:, 0:1], ALU.subtract))
            v.wait_ge(cst, 6)
            v.tensor_scalar(angs[:, 0, :], steps[:], ang[:, 0:1], None, ALU.mult)
            link(v.tensor_scalar(angs[:, 1, :], steps[:], ang[:, 2:3], TO_INT, ALU.mult, ALU.add))
            link(v.tensor_scalar(angs[:, 1, :], angs[:, 1, :], TO_INT, None, ALU.subtract))
            link(v.scalar_tensor_tensor(angs[:, 0, :], angs[:, 1, :], -TWO_PI_HI, angs[:, 0, :], ALU.mult, ALU.add))
            link(v.scalar_tensor_tensor(angs[:, 0, :], angs[:, 1, :], -TWO_PI_LO, angs[:, 0, :], ALU.mult, ALU.add))
            link(v.scalar_tensor_tensor(angs[:, 0, :], steps[:], ang[:, 1:2], angs[:, 0, :], ALU.mult, ALU.add))
            link(v.tensor_scalar(angs[:, 2, :], angs[:, 0, :], PI_DOWN, -PI_DOWN, ALU.min, ALU.max))
            v.scalar_tensor_tensor(angs[:, 3, :], angs[:, 2, :], -1.0, angs[:, 2, :], ALU.mult, ALU.max).then_inc(angled, 1)
            normalize(0, 0, xs, rstd1, xn1_made)
            v.wait_ge(sined, 2)
            shape = [P, COARSE, FINE]
            cc, cs = (coarse[:, m, 0:COARSE][:, :, None].broadcast_to(shape) for m in (0, 1))
            fc, fs = (fine[:, m, None, :].broadcast_to(shape) for m in (0, 1))
            grid = [t[:].rearrange("p (m j) -> p m j", j=FINE) for t in (cos, cos_t)]
            v.tensor_tensor(grid[0], cc, fc, ALU.mult)
            link(v.tensor_tensor(grid[1], cs, fs, ALU.mult))
            link(v.tensor_tensor(cos[:], cos[:], cos_t[:], ALU.subtract))
            v.wait_ge(powed, 4)
            link(v.tensor_tensor(pw[:, 4:5], pw[:, 3:4], sign[:], ALU.mult))
            v.wait_ge(ld_c, 32)
            v.tensor_scalar(cw[:, 0, :], ct_s[:, 0, :], sign[:], None, ALU.mult).then_inc(tabled, 1)
            v.tensor_scalar(cw[:, 1, :], ct_s[:, 1, :], -1.0, None, ALU.mult).then_inc(tabled, 1)

            def make_carry():
                v.wait_ge(cst, 11)
                link(v.tensor_scalar(carry[:], swap[:], coarse[:, 1, COARSE:COARSE + 1], None, ALU.mult))
                v.scalar_tensor_tensor(carry[:], ident[:], coarse[:, 0, COARSE:COARSE + 1], carry[:],
                                       ALU.mult, ALU.add).then_inc(tabled, 1)

            def turn(g):
                v.wait_ge(bu_done, 2 * g + 1)
                v.scalar_tensor_tensor(t1[:, g, :], HB[0][:], pw[:, 3:4], cos[:], ALU.mult, ALU.mult).then_inc(turned, 1)
                if g == 0:
                    v.wait_ge(sin_made, 2)
                    v.tensor_tensor(sin[:], sin[:], sin_t[:], ALU.add).then_inc(sin_made, 1)
                    v.wait_ge(sin_made, 3)
                v.wait_ge(bu_done, 2 * g + 2)
                v.scalar_tensor_tensor(t2[:, g, :], HB[1][:], pw[:, 4:5], sin[:], ALU.mult, ALU.mult).then_inc(turned, 1)

            def scan(g):
                v.wait_ge(turned, 2 * g + 2)
                link(v.tensor_tensor(t1[:, g, :], t1[:, g, :], t2[:, g, :], ALU.add))
                start = 0.0
                if g % SEQ_GROUPS:
                    v.wait_ge(carried, g // SEQ_GROUPS + 1)
                    start = HB[2][:, 0:1]
                v.tensor_tensor_scan(zs[:, g, :], pw[:, 2:3].broadcast_to([P, GT]), t1[:, g, :], start,
                                     ALU.mult, ALU.add).then_inc(scanned, 1)
                v.wait_ge(scanned, g + 1)
                v.tensor_tensor(t1[:, g, :], cos[:], zs[:, g, :], ALU.mult).then_inc(u1_made, 1)

            def residual(g):
                v.wait_ge(y_done, g + 1)
                v.tensor_tensor(x1[:, tiles(g), :], xs[:, tiles(g), :],
                                YF[g % 2][:].rearrange("p (i c) -> p i c", c=C), ALU.add).then_inc(x1_made, 1)
                v.wait_ge(x1_made, g + 1)
                stats(1, g, x1, stats2)

            for g in range(GROUPS + 1):
                if g < GROUPS:
                    turn(g)
                    scan(g)
                    if g == 0:
                        make_carry()
                if 2 <= g < GROUPS:
                    normalize(1, g - 2, x1, rstd2, xn2_made)
                if 1 <= g <= GROUPS:
                    residual(g - 1)
            for g in (2, 3):
                normalize(1, g, x1, rstd2, xn2_made)

            v.wait_ge(ld_sh, 32)
            v.tensor_copy(w1_parts[0][:], shw_s[:, 0:I]).then_inc(high_made, 1)
            for g in range(1, GROUPS):
                v.wait_ge(xn2t_made, g + 1)
                v.tensor_copy(x_parts[0][:, g - 1, :], xn2t[:, toks(g)]).then_inc(high_made, 1)

            wide = [P, TILES, E]
            v.wait_ge(lg_done, GROUPS)
            lgp = LB[:, 0:TILES * E].rearrange("p (i e) -> p i e", e=E)
            link(v.tensor_reduce(lmax[:], lgp, AX.X, ALU.max))
            v.tensor_tensor(lg[:], lgp, lmax[:, :, None].broadcast_to(wide), ALU.subtract).then_inc(lmaxed, 1)
            v.wait_ge(exped, 1)
            v.wait_ge(cst, CONSTS)
            left = gates
            for k in range(K):
                link(v.tensor_reduce(top[:, k, :], left[:], AX.X, ALU.max))
                link(v.tensor_tensor(pick[:], left[:], top[:, k, :, None].broadcast_to(wide), ALU.is_equal))
                link(v.tensor_tensor(pick[:], pick[:], rank_iota[:, None, :].broadcast_to(wide), ALU.mult))
                link(v.tensor_reduce(key[:], pick[:], AX.X, ALU.max))
                ins = v.tensor_tensor(chosen[:, k, :, :], pick[:], key[:, :, None].broadcast_to(wide), ALU.is_equal)
                if k == 0:
                    link(ins)
                    link(v.scalar_tensor_tensor(rest[:], chosen[:, 0, :, :], -2.0, gates[:], ALU.mult, ALU.add))
                    left = rest
                else:
                    ins.then_inc(routed, 1)
            v.wait_ge(prefixed, 2)
            ps, tot = (RB[:, n * 256:n * 256 + 256] for n in (0, 1))
            by_block = [P, E, BLOCKS]
            link(v.tensor_tensor_scan(upto[:].rearrange("p e j -> p (e j)"), restart[:].rearrange("p e j -> p (e j)"),
                                      tot, 0.0, ALU.mult, ALU.add))
            v.tensor_tensor(posn[:], upto[:], tot.rearrange("p (e j) -> p e j", e=E), ALU.subtract)
            link(v.tensor_tensor(full[:], upto[:, :, BLOCKS - 1:BLOCKS].broadcast_to([P, E, 16]),
                                 step_iota[:, None, :].broadcast_to([P, E, 16]), ALU.is_gt))
            v.tensor_tensor(posn[:], posn[:], ps.rearrange("p (e j) -> p e j", e=E), ALU.add)
            link(v.tensor_reduce(unit_count[:, 1:], full[:], AX.X, ALU.add))
            link(v.tensor_tensor_scan(units_to[:], ones[:, 0:E + 1], unit_count[:], 0.0, ALU.mult, ALU.add))
            link(v.scalar_tensor_tensor(posn[:], units_to[:, 0:E, None].broadcast_to(by_block), float(P), posn[:],
                                        ALU.mult, ALU.add))
            link(v.tensor_tensor(posn[:], posn[:], chosen[:].rearrange("p k i e -> p e (k i)"), ALU.mult))
            link(v.tensor_reduce(pos[:], posn[:].rearrange("p e j -> p j e"), AX.X, ALU.add))
            link(v.tensor_copy(pos_i[:], pos[:]))
            v.tensor_scalar(pu_i[:], pos_i[:], 7, None, ALU.logical_shift_right)
            link(v.tensor_scalar(pr_i[:], pos_i[:], P - 1, None, ALU.bitwise_and))
            v.tensor_copy(pu[:], pu_i[:])
            link(v.tensor_copy(pr[:], pr_i[:]))
            for blocks in HALVES:
                per_unit = [P, BLOCKS // 2, UNITS]
                v.tensor_tensor(in_unit[:, blocks, :], pu[:, blocks, None].broadcast_to(per_unit),
                                unit_iota[:, None, 0:UNITS].broadcast_to(per_unit), ALU.is_equal).then_inc(rows_made, 1)
            for j in range(DVE_ROWS):
                v.tensor_scalar(in_row[:, j, :], row_iota[:], pr[:, j:j + 1], None, ALU.is_equal).then_inc(posed, 1)

            def add_shared(g):
                v.wait_ge(sh2, g + 1)
                v.wait_ge(acc_made, g + 1)
                v.tensor_tensor(acc[:, tiles(g), :], acc[:, tiles(g), :],
                                SB[g][:].rearrange("p (i c) -> p i c", c=C), ALU.add).then_inc(sh_added, 1)

            v.wait_ge(inv_done, 1)
            spot_of = [LB[:, P + n * UNITS:P + n * UNITS + UNITS] for n in range(2)]
            link(v.tensor_copy(inv[:], spot_of[0]))
            link(v.scalar_tensor_tensor(dest[:], spot_of[1], float(P), inv[:], ALU.mult, ALU.add))
            link(v.tensor_scalar(tok_i[:], dest[:], float(TOKENS - P), None, ALU.add))
            v.tensor_scalar(tok_u[:], tok_i[:], TOKENS - 1, None, ALU.bitwise_and).then_inc(idx_made, 1)

            every = [1, UNITS + 2, E]
            link(v.tensor_tensor(past[:], units_to[0:1, None, 1:].broadcast_to(every),
                                 unit_iota[0:1, :, None].broadcast_to(every), ALU.is_le))
            link(v.tensor_reduce(who[:], past[:], AX.X, ALU.add))
            link(v.tensor_scalar(who[:], who[:], float(E - 1), float(WCOLS), ALU.min, ALU.mult))
            v.tensor_copy(who_i[:], who[:]).then_inc(who_made, 1)

            def set_weights(off, b):
                v.tensor_copy(wring[:, b, :], exw_s[:, bass.ds(off, WCOLS)]).then_inc(w_set, 1)

            def take_x(u, b):
                v.wait_ge(turned_x, u + 1)
                v.tensor_copy(xgt[:, b, :], TB[:, 0:P]).then_inc(xgt_made, 1)

            def take_y(u, b, landed):
                v.wait_ge(s2_done, u + 1)
                if landed is not None:
                    v.wait_ge(scattered[b], landed)
                v.tensor_tensor(ys[:, b, :], YB[:, 0:C], wring[:, b, OB2:], ALU.add).then_inc(ys_made, 1)

            regs = [v.alloc_register(f"offset{n}") for n in range(ROUND + 2)]

            def offsets(u, n):
                v.load(regs[0:n], who_i[0:1, bass.ds(u, n)])
                return [v.snap(r, min_val=0, max_val=(E - 1) * WCOLS) for r in regs[0:n]]

            def take(u, n, landed):
                if n + 1 < UNITS:
                    take_x(u + 1, (n + 1) % RING)
                if n:
                    take_y(u - 1, (n - 1) % RING, landed)

            def refill(u, n, off):
                if n:
                    v.wait_ge(ys_made, u)
                set_weights(off, (n + 2) % RING)

            def landed(n):
                return 16 * ((n - 1) // RING) if n > RING else None

            v.wait_ge(ld_ex, 32)
            v.wait_ge(who_made, 1)
            offs = offsets(0, ROUND + 2)
            set_weights(offs[0], 0)
            take_x(0, 0)
            set_weights(offs[1], 1)
            take(0, 0, None)
            add_shared(2)
            add_shared(1)
            refill(0, 0, offs[2])
            add_shared(0)
            for u in range(1, ROUND):
                take(u, u, landed(u))
                refill(u, u, offs[u + 2])
                if u == 1:
                    link(v.scalar_tensor_tensor(spare[:], dest[:], 0.0, spare_iota[:], ALU.is_equal, ALU.mult))
                    link(v.scalar_tensor_tensor(dest[:], dest[:], -float(P), spare[:], ALU.add, ALU.add))
                    v.tensor_copy(dest_u[:], dest[:]).then_inc(idx_made, 1)
                elif u == 4:
                    v.tensor_tensor(wtmp[:, 0, :], top[:, 1, :], top[:, 0, :], ALU.subtract)
                    link(v.tensor_reduce(gsum[:], gates[:], AX.X, ALU.add))
                    link(v.reciprocal(ginv[:], gsum[:]))
                    v.tensor_tensor(wtmp[:, 0, :], wtmp[:, 0, :], ginv[:], ALU.mult).then_inc(wdiff, 1)
            with v.Fori(1, ROUNDS) as r:
                for n in range(ROUND):
                    per_round = 16 * ROUND // RING
                    take(r * ROUND + n, ROUND + n, r * per_round + (landed(ROUND + n) - per_round))
                    if n == 0:
                        offs = offsets(r * ROUND + 2, ROUND)
                    refill(r * ROUND + n, ROUND + n, offs[n])
            for u in range(ROUND * ROUNDS, UNITS):
                take(u, u, landed(u))
                if u == ROUND * ROUNDS:
                    offs = offsets(u + 2, UNITS - u - 2)
                if u + 2 < UNITS:
                    refill(u, u, offs[u - ROUND * ROUNDS])
            v.wait_ge(exped, 2)
            v.tensor_scalar(wk[:, 0, :], wtmp[:, 1, :], -0.5, 0.5, ALU.mult, ALU.add)
            v.tensor_scalar(wk[:, 1, :], wtmp[:, 1, :], 0.5, 0.5, ALU.mult, ALU.add).then_inc(wk_made, 1)
            take_y(UNITS - 1, (UNITS - 1) % RING, landed(UNITS))
            v.wait_ge(wk_made, 1)

            for g in range(GROUPS):
                if g == GROUPS - 2:
                    add_shared(GROUPS - 1)
                if g == GROUPS - 1:
                    v.wait_ge(weighted, g + 1)
                    v.wait_ge(sh_added, GROUPS)
                    link(v.tensor_tensor(acc[:, tiles(g), :], acc[:, tiles(g), :], yk[0][:, tiles(g), :], ALU.add))
                v.wait_ge(ld_y[1][g], 16)
                for i in range(TG * g, TG * g + TG):
                    ins = v.scalar_tensor_tensor(acc[:, i, :], yk[1][:, i, :], wk[:, 1, i:i + 1], acc[:, i, :],
                                                 ALU.mult, ALU.add)
                ins.then_inc(added, 1)

        @block.tensor
        def _(pe):
            def transposes(dst, src, g, ready, signal):
                pe.wait_ge(ready, g + 1)
                for i in range(TG):
                    ins = pe.transpose(dst[:, i * P:i * P + P], src[:, TG * g + i, :], ident[:])
                ins.then_inc(signal, 1)

            def first_turn(g):
                if g:
                    pe.wait_ge(xnt_made, g)
                transposes(TB, xn, g, xn1_made, t1_done)

            def second_turn(g):
                if g:
                    pe.wait_ge(xn2t_made, g)
                transposes(YB, xn, g, xn2_made, t2_done)

            def inputs(g):
                pe.wait_ge(xnt_made, g + 1)
                for n in range(2):
                    if g:
                        pe.wait_ge(turned, 2 * (g - 1) + n + 1)
                    pe.matmul(HB[n][:], bt_s[:, n, :], xnt[:, toks(g)], start=True, stop=True).then_inc(bu_done, 1)

            def y_part(g, i):
                return YF[g % 2][:, i * C:i * C + C]

            def direct(g):
                if g >= 2:
                    pe.wait_ge(x1_made, g - 1)
                if g == 0:
                    pe.wait_ge(ld_c, 32)
                for i in range(TG):
                    pe.matmul(y_part(g, i), xnt[:, GT * g + i * P:GT * g + i * P + P], dt_s[:],
                              start=(i == 0), stop=False)

            def outputs(g):
                if g == 0:
                    pe.wait_ge(tabled, 2)
                for n, (part, made) in enumerate(((t1, u1_made), (t2, u2_made))):
                    pe.wait_ge(made, g + 1)
                    for i in range(TG):
                        ins = pe.matmul(y_part(g, i), part[:, g, i * P:i * P + P], cw[:, n, :],
                                        start=False, stop=(n == 1 and i == TG - 1))
                ins.then_inc(y_done, 1)

            def router(g):
                pe.wait_ge(xn2t_made, g + 1)
                if g == 0:
                    pe.wait_ge(ld_r, 48)
                elif g == 1:
                    pe.wait_ge(xnt_made, GROUPS)
                else:
                    pe.wait_ge(h1_made, g - 1)
                pe.matmul(RH[g % 2][0:R, :], wr1_s[:], xn2t[:, toks(g)], start=True, stop=True).then_inc(h1_done, 1)

            def logits(g):
                if g == 0:
                    pe.wait_ge(zeroed, 2)
                    pe.wait_ge(x1_made, GROUPS)
                pe.wait_ge(h1_made, g + 1)
                for i in range(TG * g, TG * g + TG):
                    ins = pe.matmul(LB[:, i * E:i * E + E], h1[:, i * P:i * P + P], wr2_s[:], start=True, stop=True)
                ins.then_inc(lg_done, 1)

            def turn_over(g):
                if g == 0:
                    pe.wait_ge(tabled, 3)
                pe.wait_ge(scanned, g + 1)
                pe.matmul(HB[2][:, 0:1], carry[:], zs[:, g, GT - 1:GT], start=True, stop=True).then_inc(carried, 1)

            def shared_1(n):
                g, c = n // IC, n % IC
                if n == 0:
                    pe.wait_ge(ld_sh, 32)
                if n >= IC * (GROUPS - 1):
                    pe.wait_ge(h_made, IC * UNITS)
                if n >= 3:
                    pe.wait_ge(sh_act, n - 2)
                elif n < 2:
                    pe.wait_ge(turned, 2 * (GROUPS - 1) + n + 1)
                else:
                    pe.wait_ge(scanned, GROUPS)
                if g == 0:
                    ins = pe.matmul(HB[n % 3][:], shw_s[:, c * P:c * P + P], xn2t[:, toks(g)], start=True, stop=True)
                else:
                    pe.wait_ge(high_made, g + 1)
                    pe.wait_ge(low_made, g + 1)
                    for m, (w, x) in enumerate(((0, 0), (0, 1), (1, 0))):
                        ins = pe.matmul(HB[n % 3][:], w1_parts[w][:, c * P:c * P + P],
                                        x_parts[x][:, g - 1, :], start=(m == 0), stop=(m == 2))
                ins.then_inc(sh1, 1)

            def shared_2(g, tiles=range(TG)):
                pe.wait_ge(sh_act, IC * (g + 1))
                if g == 0:
                    pe.wait_ge(x1_made, GROUPS)
                elif g == 1:
                    pe.wait_ge(xn2t_made, GROUPS)
                for i in tiles:
                    for c in range(IC):
                        ins = pe.matmul(SB[g][:, i * C:i * C + C], hs[:, g % 2, c, i * P:i * P + P],
                                        shw_s[:, OW2 + c * C:OW2 + c * C + C], start=(c == 0), stop=(c == IC - 1))
                if tiles[-1] == TG - 1:
                    ins.then_inc(sh2, 1)

            pe.wait_ge(zeroed, 1)
            with pe.Fori(0, WARM_UP):
                for _ in range(4):
                    pe.matmul(LB[:], zeros[:, 0:P], zeros[:], start=True, stop=True)

            pe.wait_ge(cst, 8)
            first_turn(0)
            pe.wait_ge(ld_b, 16)
            inputs(0)
            first_turn(1)
            direct(0)
            inputs(1)
            turn_over(0)
            outputs(0)
            direct(1)
            first_turn(2)
            inputs(2)
            direct(2)
            outputs(1)
            first_turn(3)
            inputs(3)
            direct(3)
            turn_over(2)
            second_turn(0)
            outputs(2)
            router(0)
            shared_1(0)
            outputs(3)
            second_turn(1)
            shared_1(1)
            router(1)
            logits(0)
            shared_1(2)
            second_turn(2)
            logits(1)
            second_turn(3)
            router(2)
            router(3)
            logits(2)
            logits(3)
            for n in range(3, 6):
                shared_1(n)
            shared_2(0, range(2))

            pe.wait_ge(cst, CONSTS)
            pe.wait_ge(routed, 1)
            rows = chosen[:].rearrange("p k i e -> p e (k i)")
            for n, lhs in enumerate((before, ones)):
                pe.matmul(RB[:, n * 256:n * 256 + 256], lhs[:], rows, start=True, stop=True).then_inc(prefixed, 1)
            for n in (6, 7):
                shared_1(n)
            shared_2(0, range(2, TG))
            for n in (8, 9):
                shared_1(n)
            shared_2(1, range(2))
            for j in range(BLOCKS):
                if j % (BLOCKS // 2) == 0:
                    half = j // (BLOCKS // 2)
                    pe.wait_ge(parts_made, half + 1)
                    pe.wait_ge(blocks_made, half + 1)
                if j < DVE_ROWS:
                    pe.wait_ge(posed, j + 1)
                else:
                    pe.wait_ge(posed_by_pool, j + 1 - DVE_ROWS)
                ins = pe.matmul(LB[:, P:P + 2 * UNITS], in_row[:, j, :], from_who[:, j, :, :].rearrange("p n u -> p (n u)"),
                                start=(j == 0), stop=(j == BLOCKS - 1))
                if j == 7 or j == 15:
                    shared_1(10 + j // 8)
                if j == 15:
                    shared_2(1, range(2, 3))
            ins.then_inc(inv_done, 1)
            shared_2(1, range(3, TG))

            def turn_x(u, n, landed):
                pe.wait_ge(gathered[n % AHEAD], landed)
                if n:
                    pe.wait_ge(xgt_made, u)
                else:
                    pe.wait_ge(h1_made, GROUPS)
                pe.transpose(TB[:, 0:P], xg[:, n % AHEAD, :], ident[:]).then_inc(turned_x, 1)

            def up(u, n):
                b = n % RING
                if n == 0:
                    pe.wait_ge(sh_act, IC * (GROUPS - 1))
                elif n == 1:
                    pe.wait_ge(sh_added, 1)
                elif n == 2:
                    pe.wait_ge(sh_added, 3)
                pe.wait_ge(w_set, u + 1)
                pe.wait_ge(xgt_made, u + 1)
                for c in range(IC):
                    ins = pe.matmul(HU[b][c // 2][:, c % 2 * P:c % 2 * P + P], wring[:, b, c * P:c * P + P],
                                    xgt[:, b, :], start=True, stop=True)
                    if c % 2:
                        ins.then_inc(s1_done, 1)

            def down(u, n):
                b = n % RING
                if n:
                    pe.wait_ge(ys_made, u)
                else:
                    pe.wait_ge(sh_added, 2)
                for c in range(IC):
                    pe.wait_ge(h_made, u * IC + c + 1)
                    ins = pe.matmul(YB[:, 0:C], he[:, b, c, :], wring[:, b, OW2 + c * C:OW2 + c * C + C],
                                    start=(c == 0), stop=(c == IC - 1))
                ins.then_inc(s2_done, 1)

            def unit(u, n, landed):
                if n + 1 < UNITS:
                    turn_x(u + 1, n + 1, landed)
                up(u, n)
                if n:
                    down(u - 1, n - 1)

            def landed(n):
                return 16 * (n // AHEAD + 1)

            shared_2(2)
            turn_x(0, 0, landed(0))
            for u in range(ROUND):
                unit(u, u, landed(u + 1))
            with pe.Fori(1, ROUNDS) as r:
                for n in range(ROUND):
                    per_round = 16 * ROUND // AHEAD
                    unit(r * ROUND + n, ROUND + n, r * per_round + (landed(ROUND + n + 1) - per_round))
            for u in range(ROUND * ROUNDS, UNITS):
                unit(u, u, landed(u + 1))
            down(UNITS - 1, UNITS - 1)

            for n in range(IC * (GROUPS - 1), IC * GROUPS):
                shared_1(n)
            shared_2(GROUPS - 1)


def kernel(**inputs):
    import numpy as np
    import concourse.bacc as bacc
    from concourse.bass_utils import run_bass_kernel_spmd

    a = {name.replace("L0_", ""): np.asarray(value) for name, value in inputs.items()}

    def down(w):
        return w.reshape(IC, P, C).transpose(1, 0, 2).reshape(P, IC * C)

    arrays = {
        "x": a["attn_x"],
        "prm": np.tile(np.stack([a["attn_nu_log"], a["attn_theta_log"], a["attn_gamma_log"]], 1), (2, 1)),
        "bt": np.stack([np.concatenate([a["attn_B_re"], a["attn_B_im"]]).T,
                        np.concatenate([a["attn_B_im"], a["attn_B_re"]]).T], 1),
        "ct": np.stack([np.concatenate([a["attn_C_re"], a["attn_C_im"]], 1).T,
                        np.concatenate([a["attn_C_im"], a["attn_C_re"]], 1).T], 1),
        "dt": a["attn_D"].T,
        "wr1": a["ffn_Wr1"],
        "br1": a["ffn_br1"][:, None],
        "wr2": np.concatenate([a["ffn_Wr2"], a["ffn_br2"][None]]),
        "shw": np.concatenate([a["ffn_Ws1"], down(a["ffn_Ws2"]), a["ffn_bs1"].reshape(IC, P).T], 1),
        "bs2": a["ffn_bs2"][None],
        "exw": np.stack([np.concatenate([a["ffn_We1"][e], down(a["ffn_We2"][e]), a["ffn_be1"][e].reshape(IC, P).T], 1)
                         for e in range(E)], 1),
        "be2": a["ffn_be2"][None],
    }
    nc = bacc.Bacc("TRN2", target_bir_lowering=False, num_devices=1)
    feeds, aps = {}, []
    for name, value in arrays.items():
        feeds[f"in_{name}"] = np.ascontiguousarray(value)
        aps.append(nc.dram_tensor(f"in_{name}", value.shape, mybir.dt.from_np(value.dtype), kind="ExternalInput").ap())
    shape = a["attn_x"].shape
    aps.append(nc.dram_tensor("out_x", shape, F32, kind="ExternalOutput").ap())
    seq_moe_kernel(nc, *aps)
    r = run_bass_kernel_spmd(nc, [feeds], core_ids=[0])
    return r.results[0]["out_x"]
```
